# Optimizing a Trainium2 kernel written in Bass

```python
import numpy as np
import jax
import jax.numpy as jnp

def _softmax(x, axis=-1):
    return jax.nn.softmax(x, axis=axis)

def _gelu(x):
    return jax.nn.gelu(x, approximate=True)

def _silu(x):
    return jax.nn.silu(x)

def _sigmoid(x):
    return jax.nn.sigmoid(x)

def _layernorm(x, axis=-1, eps=1e-05):
    m = jnp.mean(x, axis=axis, keepdims=True)
    v = jnp.var(x, axis=axis, keepdims=True)
    return (x - m) / jnp.sqrt(v + eps)

def _scatter_add(tgt, idx, src, axis=0):
    return tgt.at[idx].add(src)

def _segment_sum(src, seg, n):
    return jax.ops.segment_sum(src, seg, n)
kernel_name = 'mk_flamingo_gated_d2_seqx_r8_9a874c'

def setup_inputs(seed: int=0):
    np.random.seed(seed)
    _w = jnp.asarray

    def _rec_inputs():
        import jax
        import jax.numpy as jnp
        _rk = jax.random.key(seed)
        x = 7.22e-05 + 1 * jax.random.normal(jax.random.fold_in(_rk, 1), (16, 64, 256), jnp.float32)
        _lenS = 64 - jax.random.randint(jax.random.fold_in(_rk, 7), (16,), 0, max(1, 64 // 4) + 1, jnp.int32)
        _lenS2 = 64 - jax.random.randint(jax.random.fold_in(_rk, 8), (16,), 0, max(1, 64 // 4) + 1, jnp.int32)
        _ctx_512P = jax.random.normal(jax.random.fold_in(_rk, 11), (16, 16, 64), jnp.float32)
        _ctx_512c = jax.random.dirichlet(jax.random.fold_in(_rk, 511), 0.3 * jnp.ones((16,), jnp.float32), (16, 64))
        _ctx_512t = jnp.einsum('bsk,bkd->bsd', _ctx_512c, _ctx_512P)
        _ctx_512t = _ctx_512t * jax.lax.rsqrt(jnp.mean(jnp.square(_ctx_512t)) + 1e-12) * 0.953939
        ctx_512 = -0.000514642 + 1.00011 * (_ctx_512t + 0.3 * jax.random.normal(jax.random.fold_in(_rk, 611), (16, 64, 64), jnp.float32))
        _g = jax.random.normal(jax.random.fold_in(_rk, 9001), (2, 2), jnp.float32)
        _g = jnp.sign(_g) * jnp.maximum(jnp.abs(_g), 1.0) + (_g == 0) * 1.0
        g_xattn = _g[0]
        g_ffn = _g[1]
        return (x, ctx_512, g_xattn, g_ffn)
    x, ctx_512, g_xattn, g_ffn = _rec_inputs()

    def _L0_xattn_setup():
        import jax, jax.numpy as jnp
        import numpy as np
        import math
        NUM_Q_HEADS = 32
        NUM_KV_HEADS = 8
        key = jax.random.key(seed)
        k1, k2, k3 = jax.random.split(key, 3)
        B, S, E = (2, 256, 256)
        kv_E = NUM_KV_HEADS * (E // NUM_Q_HEADS)
        q = jax.random.normal(k1, (B, S, E), dtype=jnp.float32)
        k = jax.random.normal(k2, (B, S, kv_E), dtype=jnp.float32)
        v = jax.random.normal(k3, (B, S, kv_E), dtype=jnp.float32)
        return {'q': q, 'k': k, 'v': v}
    _L0_xattn_all = _L0_xattn_setup()
    _L0_xattn_in = {k: v for k, v in _L0_xattn_all.items() if k in ()}
    del _L0_xattn_all

    def _L0_ffn_setup():
        import jax, jax.numpy as jnp
        import numpy as np
        DIM = 256
        HID = 704
        ZERO_POINT = 128.0

        def _qlinear(x, wq, scale):
            W = (wq.astype(jnp.float32) - ZERO_POINT) * scale[:, None]
            return jnp.einsum('bsd,hd->bsh', x, W)
        key = jax.random.key(seed)
        ks = jax.random.split(key, 7)
        B, S = (4, 256)
        sg = jax.random.uniform(ks[1], (HID,)) * (0.02 / np.sqrt(DIM)) + 0.0001
        su = jax.random.uniform(ks[3], (HID,)) * (0.02 / np.sqrt(DIM)) + 0.0001
        sd = jax.random.uniform(ks[5], (DIM,)) * (0.02 / np.sqrt(HID)) + 0.0001
        return {'x': jax.random.normal(ks[0], (B, S, DIM), dtype=jnp.float32), 'wq_gate': jax.random.randint(ks[2], (HID, DIM), 0, 32, dtype=jnp.int32), 's_gate': sg, 'wq_up': jax.random.randint(ks[4], (HID, DIM), 0, 32, dtype=jnp.int32), 's_up': su, 'wq_down': jax.random.randint(ks[6], (DIM, HID), 0, 32, dtype=jnp.int32), 's_down': sd}
    _L0_ffn_all = _L0_ffn_setup()
    _L0_ffn_in = {k: v for k, v in _L0_ffn_all.items() if k in ('wq_gate', 's_gate', 'wq_up', 's_up', 'wq_down', 's_down')}
    del _L0_ffn_all

    def _L1_xattn_setup():
        import jax, jax.numpy as jnp
        import numpy as np
        import math
        D_MODEL = 256
        N_HEADS = 16
        N_GROUPS = 4
        HEADS_PER_GROUP = N_HEADS // N_GROUPS
        HEAD_DIM = D_MODEL // N_HEADS
        B, S = (2, 256)
        key = jax.random.key(seed)
        k1, k2, k3, k4, k5 = jax.random.split(key, 5)
        q = jax.random.normal(k1, (B, S, D_MODEL), dtype=jnp.float32)
        k = jax.random.normal(k2, (B, S, N_GROUPS * HEAD_DIM), dtype=jnp.float32)
        v = jax.random.normal(k3, (B, S, N_GROUPS * HEAD_DIM), dtype=jnp.float32)
        lim = 1.0 / math.sqrt(D_MODEL)
        Wc = jax.random.uniform(k4, (D_MODEL, D_MODEL), minval=-lim, maxval=lim, dtype=jnp.float32)
        bc = jax.random.uniform(k5, (D_MODEL,), minval=-lim, maxval=lim, dtype=jnp.float32)
        return {'q': q, 'k': k, 'v': v, 'Wc': Wc, 'bc': bc}
    _L1_xattn_all = _L1_xattn_setup()
    _L1_xattn_in = {k: v for k, v in _L1_xattn_all.items() if k in ('Wc', 'bc')}
    del _L1_xattn_all

    def _L1_ffn_setup():
        import jax, jax.numpy as jnp
        import numpy as np
        TOP_K = 8

        def _masked_routing(router_logits):
            T, E = router_logits.shape
            sel_w, sel_e = jax.lax.top_k(router_logits, TOP_K)
            sel_w = jax.nn.softmax(sel_w.astype(jnp.float32), axis=1)
            rows = jnp.arange(T)[:, None]
            masked = jnp.zeros((T, E), dtype=jnp.float32).at[rows, sel_e].set(sel_w)
            count = jnp.zeros((E,), dtype=jnp.int32).at[sel_e.reshape(-1)].add(1)
            return (masked, count)
        key = jax.random.key(seed)
        k1, k2, k3, k4, k5 = jax.random.split(key, 5)
        B, S, H, E, I = (1, 256, 256, 32, 96)
        return {'hidden_states': jax.random.normal(k1, (B, S, H), dtype=jnp.float32), 'gate_w': jax.random.normal(k2, (E, H), dtype=jnp.float32) * H ** (-0.5), 'w_gate_proj': jax.random.normal(k3, (E, I, H), dtype=jnp.float32) * H ** (-0.5), 'w_up_proj': jax.random.normal(k4, (E, I, H), dtype=jnp.float32) * H ** (-0.5), 'w_down_proj': jax.random.normal(k5, (E, H, I), dtype=jnp.float32) * I ** (-0.5)}
    _L1_ffn_all = _L1_ffn_setup()
    _L1_ffn_in = {k: v for k, v in _L1_ffn_all.items() if k in ('gate_w', 'w_gate_proj', 'w_up_proj', 'w_down_proj')}
    del _L1_ffn_all
    return {'x': x, 'ctx_512': ctx_512, 'g_xattn': g_xattn, 'g_ffn': g_ffn, 'L0_ffn_wq_gate': _L0_ffn_in['wq_gate'], 'L0_ffn_s_gate': _L0_ffn_in['s_gate'], 'L0_ffn_wq_up': _L0_ffn_in['wq_up'], 'L0_ffn_s_up': _L0_ffn_in['s_up'], 'L0_ffn_wq_down': _L0_ffn_in['wq_down'], 'L0_ffn_s_down': _L0_ffn_in['s_down'], 'L1_xattn_Wc': _L1_xattn_in['Wc'], 'L1_xattn_bc': _L1_xattn_in['bc'], 'L1_ffn_gate_w': _L1_ffn_in['gate_w'], 'L1_ffn_w_gate_proj': _L1_ffn_in['w_gate_proj'], 'L1_ffn_w_up_proj': _L1_ffn_in['w_up_proj'], 'L1_ffn_w_down_proj': _L1_ffn_in['w_down_proj']}

def reference(x, ctx_512, g_xattn, g_ffn, L0_ffn_wq_gate, L0_ffn_s_gate, L0_ffn_wq_up, L0_ffn_s_up, L0_ffn_wq_down, L0_ffn_s_down, L1_xattn_Wc, L1_xattn_bc, L1_ffn_gate_w, L1_ffn_w_gate_proj, L1_ffn_w_up_proj, L1_ffn_w_down_proj):
    import jax
    import jax.numpy as jnp

    def _L0_xattn_ref(q, k, v):
        import jax, jax.numpy as jnp
        import numpy as np
        import math
        NUM_Q_HEADS = 32
        NUM_KV_HEADS = 8
        B, S, E = q.shape
        H, KV = (NUM_Q_HEADS, NUM_KV_HEADS)
        D = E // H
        G = H // KV
        scale = math.sqrt(D)
        qh = q.reshape(B, S, KV, G, D).transpose(0, 2, 3, 1, 4)
        kh = k.reshape(B, S, KV, D).transpose(0, 2, 1, 3)
        vh = v.reshape(B, S, KV, D).transpose(0, 2, 1, 3)
        scores = jnp.einsum('bkgsd,bktd->bkgst', qh, kh) / scale
        weights = jax.nn.softmax(scores, axis=-1)
        out = jnp.einsum('bkgst,bktd->bkgsd', weights, vh)
        return out.transpose(0, 3, 1, 2, 4).reshape(B, S, E)

    def _L0_ffn_ref(x, wq_gate, s_gate, wq_up, s_up, wq_down, s_down):
        import jax, jax.numpy as jnp
        import numpy as np
        DIM = 256
        HID = 704
        ZERO_POINT = 128.0

        def _qlinear(x, wq, scale):
            W = (wq.astype(jnp.float32) - ZERO_POINT) * scale[:, None]
            return jnp.einsum('bsd,hd->bsh', x, W)
        gate = _qlinear(x, wq_gate, s_gate)
        gate = jax.nn.silu(gate)
        up = _qlinear(x, wq_up, s_up)
        return _qlinear(gate * up, wq_down, s_down)

    def _L1_xattn_ref(q, k, v, Wc, bc):
        import jax, jax.numpy as jnp
        import numpy as np
        import math
        D_MODEL = 256
        N_HEADS = 16
        N_GROUPS = 4
        HEADS_PER_GROUP = N_HEADS // N_GROUPS
        HEAD_DIM = D_MODEL // N_HEADS
        B, S = (2, 256)
        b, s, _ = q.shape
        qh = q.reshape(b, s, N_GROUPS, HEADS_PER_GROUP, HEAD_DIM).transpose(0, 2, 3, 1, 4)
        kh = k.reshape(b, s, N_GROUPS, HEAD_DIM).transpose(0, 2, 1, 3)
        vh = v.reshape(b, s, N_GROUPS, HEAD_DIM).transpose(0, 2, 1, 3)
        scale = 1.0 / math.sqrt(HEAD_DIM)
        scores = jnp.einsum('bghsd,bgtd->bghst', qh, kh) * scale
        probs = jax.nn.softmax(scores, axis=-1)
        out = jnp.einsum('bghst,bgtd->bghsd', probs, vh)
        out = out.transpose(0, 3, 1, 2, 4).reshape(b, s, D_MODEL)
        return out @ Wc.T + bc

    def _L1_ffn_ref(hidden_states, gate_w, w_gate_proj, w_up_proj, w_down_proj):
        import jax, jax.numpy as jnp
        import numpy as np
        TOP_K = 8

        def _masked_routing(router_logits):
            T, E = router_logits.shape
            sel_w, sel_e = jax.lax.top_k(router_logits, TOP_K)
            sel_w = jax.nn.softmax(sel_w.astype(jnp.float32), axis=1)
            rows = jnp.arange(T)[:, None]
            masked = jnp.zeros((T, E), dtype=jnp.float32).at[rows, sel_e].set(sel_w)
            count = jnp.zeros((E,), dtype=jnp.int32).at[sel_e.reshape(-1)].add(1)
            return (masked, count)
        B, S, H = hidden_states.shape
        x = hidden_states.reshape(-1, H)
        router_logits = x @ gate_w.T
        masked_w, _count = _masked_routing(router_logits)
        g = jnp.einsum('th,eih->tei', x, w_gate_proj)
        u = jnp.einsum('th,eih->tei', x, w_up_proj)
        h = jax.nn.silu(g) * u
        h = h * masked_w[:, :, None]
        out = jnp.einsum('tei,ehi->th', h, w_down_proj)
        return out.reshape(B, S, H)
    x = x + jnp.tanh(g_xattn[0]) * _L0_xattn_ref(_layernorm(x, axis=-1), ctx_512, ctx_512)
    x = x + jnp.tanh(g_ffn[0]) * _L0_ffn_ref(_layernorm(x, axis=-1), L0_ffn_wq_gate, L0_ffn_s_gate, L0_ffn_wq_up, L0_ffn_s_up, L0_ffn_wq_down, L0_ffn_s_down)
    x = x + jnp.tanh(g_xattn[1]) * _L1_xattn_ref(_layernorm(x, axis=-1), ctx_512, ctx_512, L1_xattn_Wc, L1_xattn_bc)
    x = x + jnp.tanh(g_ffn[1]) * _L1_ffn_ref(_layernorm(x, axis=-1), L1_ffn_gate_w, L1_ffn_w_gate_proj, L1_ffn_w_up_proj, L1_ffn_w_down_proj)
    return x

_drawn_inputs = setup_inputs


def setup_inputs(seed=0):
    import zlib

    import numpy as np

    out = dict(_drawn_inputs(seed))
    spreads = {'g_ffn': (-1.0, 0.6)}
    factors = {'L0_ffn_s_gate': 8.0, 'L0_ffn_s_up': 8.0, 'L0_ffn_s_down': 8.0, 'L1_xattn_bc': 7.885}
    for name, (base, spread) in spreads.items():
        noise = np.random.default_rng([zlib.crc32(name.encode()), seed]).standard_normal(out[name].shape)
        drawn = base * np.exp(spread * noise) if base else spread * noise
        out[name] = jnp.asarray(drawn.astype(out[name].dtype))
    for name, factor in factors.items():
        out[name] = (out[name] * factor).astype(out[name].dtype)
    return out
```

```python
from contextlib import ExitStack

import concourse.bass as bass
from concourse import mybir

ALU = mybir.AluOpType
ACT = mybir.ActivationFunctionType
AX = mybir.AxisListType
F32 = mybir.dt.float32
F32R = mybir.dt.float32r
I32 = mybir.dt.int32

P = 128
DM = 256
KC = DM // P
TT = 8
TOK = TT * P
BATCH = 16
SEQ = 64
KEYS = 64
G = 4
UNITS = 4
BLK = 512
NBLK = TOK // BLK
EXPERTS = 32
INNER = 96
TOPK = 8
EPQ = 4
CPQ = EPQ * INNER // P
MOE_CHUNKS = EXPERTS * INNER // P
WPACK = 3 * DM
WRING = 3
EPS = 1e-5
ZERO_POINT = 128.0
HIDDEN = 704
FFN_CHUNKS = (HIDDEN + P - 1) // P
NEG = -3.0e38


class Chain:

    def __init__(self, eng, sem):
        self.eng, self.sem, self.base, self.n = eng, sem, 0, 0

    def at(self, base):
        self.base, self.n = base, 0

    def link(self, ins):
        ins.then_inc(self.sem, 1)
        self.n += 1
        self.eng.wait_ge(self.sem, self.base + self.n)


class Attention:

    def __init__(self, layer, kv_heads, sb, sem):
        self.layer, self.hk = layer, kv_heads
        self.d = DM // G // kv_heads
        self.ns = kv_heads * KEYS
        self.npair = kv_heads // 2
        self.vw = 2 * self.d + 2
        self.scale = float(self.d) ** -0.5
        n = f"a{layer}_"
        self.kbd = sb(n + "kbd", [P, BATCH, self.ns])
        self.vbd = sb(n + "vbd", [P, BATCH, self.npair, self.vw])
        self.k_zeroed = sem(n + "k_zeroed")
        self.k_loaded = sem(n + "k_loaded")
        self.v_ready = sem(n + "v_ready")
        self.var_ready = sem(n + "var_ready")
        self.rstd_ready = sem(n + "rstd_ready")
        self.xn_ready = sem(n + "xn_ready")
        self.q_transposed = sem(n + "q_transposed")
        self.q_ready = sem(n + "q_ready")
        self.scored = sem(n + "scored")
        self.sub_done = sem(n + "sub_done")
        self.p_ready = sem(n + "p_ready")
        self.pt_done = sem(n + "pt_done")
        self.pts_ready = sem(n + "pts_ready")
        self.av_done = sem(n + "av_done")
        self.y_done = sem(n + "y_done")
        self.x_done = sem(n + "x_done")
        self.yt_done = sem(n + "yt_done")
        self.yts_ready = sem(n + "yts_ready")
        self.proj_done = sem(n + "proj_done")
        self.dve_chain = sem(n + "dve_chain")


class Mlp:

    def __init__(self, layer, chunks, per_body, sem):
        self.layer, self.chunks, self.per_body = layer, chunks, per_body
        n = f"m{layer}_"
        self.var_ready = sem(n + "var_ready")
        self.rstd_ready = sem(n + "rstd_ready")
        self.xn_ready = sem(n + "xn_ready")
        self.xt_done = sem(n + "xt_done")
        self.xtf_ready = sem(n + "xtf_ready")
        self.xt_split = sem(n + "xt_split")
        self.wf_ready = sem(n + "wf_ready")
        self.wh_ready = sem(n + "wh_ready")
        self.w_split = sem(n + "w_split")
        self.g_done = sem(n + "g_done")
        self.u_done = sem(n + "u_done")
        self.s_ready = sem(n + "s_ready")
        self.t_done = sem(n + "t_done")
        self.h_full = self.t_done if layer == 0 else sem(n + "h_full")
        self.hh_ready = sem(n + "hh_ready")
        self.h_split = sem(n + "h_split")
        self.dn_done = sem(n + "dn_done")
        self.ot_ready = sem(n + "ot_ready")
        self.back_done = sem(n + "back_done")
        self.x_done = sem(n + "x_done")
        self.dve_chain = sem(n + "dve_chain")
        self.logits_done = sem(n + "logits_done")
        self.route_chain = sem(n + "route_chain")
        self.d_ready = sem(n + "d_ready")
        self.e_ready = sem(n + "e_ready")
        self.w_ready = sem(n + "w_ready")
        self.wt_done = sem(n + "wt_done")
        self.wts_ready = sem(n + "wts_ready")
        self.w_stored = sem(n + "w_stored")
        self.m_loaded = sem(n + "m_loaded")
        self.w_loaded = [sem(n + f"w_loaded{i}") for i in range(2)]


def build(nc, x_in, ctx_t, ctx_in, g_xattn, g_ffn, w0, s_gate, s_up, s_down, wc_t, bc, gate_t, w1, ident_in,
          mask_dram, out, stages=4):
    with ExitStack() as stack:
        def sb(name, shape, dt=F32):
            return stack.enter_context(nc.sbuf_tensor(name, shape, dt))

        def sem(name):
            return stack.enter_context(nc.semaphore(name))

        A = [Attention(0, 8, sb, sem), Attention(1, 4, sb, sem)]
        M = [Mlp(0, FFN_CHUNKS, FFN_CHUNKS, sem), Mlp(1, MOE_CHUNKS, 2 * CPQ, sem)]

        x = sb("x", [P, TT, DM])
        ident = sb("ident", [P, P])
        ctx_v = sb("ctx_v", [P, BATCH, 64])
        tg = sb("tg", [P, 4])
        sg = sb("sg", [P, FFN_CHUNKS])
        su = sb("su", [P, FFN_CHUNKS])
        sd = sb("sd", [P, KC])
        sdt = sb("sdt", [P, KC])
        wc = sb("wc", [P, KC, DM])
        bcr = sb("bcr", [1, DM])
        ones = sb("ones", [1, P])
        gw = sb("gw", [P, KC, EXPERTS])
        stats = sb("stats", [P, TT, 6])
        mv = sb("mv", [P, TT, 2])
        ve = sb("ve", [P, TT])
        neghalf = sb("neghalf", [P, TT])
        rstd = sb("rstd", [P, TT])
        xn = sb("xn", [P, DM])
        qt = sb("qt", [P, 2, G // 2, 2, SEQ])
        mx = sb("mx", [P, 2, 8])
        dt_ = sb("dt", [P, 2, 512])
        pt = sb("pt", [P, 2, 512])
        pts = sb("pts", [P, 2, 4, P])
        rc = sb("rc", [P, 2, 8])
        yt = sb("yt", [P, DM])
        yts = sb("yts", [P, KC, P])
        xtf = sb("xtf", [P, KC, P])
        xh = sb("xh", [P, KC, TOK], F32R)
        xl = sb("xl", [P, KC, TOK], F32R)
        wraw = sb("wraw", [P, 2, WPACK])
        wrawi = wraw[:].bitcast(I32)
        wf = sb("wf", [P, 2, WPACK])
        wh = sb("wh", [P, WRING, WPACK], F32R)
        wl = sb("wl", [P, WRING, WPACK], F32R)
        s_t = sb("s_t", [P, 2, BLK])
        t_t = sb("t_t", [P, BLK])
        h_t = sb("h_t", [P, 2, BLK])
        hh = sb("hh", [P, 2, BLK], F32R)
        hl = sb("hl", [P, 2, BLK], F32R)
        ot = sb("ot", [P, KC, TOK])
        top = sb("top", [P, TT, TOPK])
        lg = sb("lg", [P, TT, EXPERTS])
        rep = sb("rep", [P, TT, EXPERTS])
        ew = sb("ew", [P, TT, EXPERTS])
        esum = sb("esum", [P, TT])
        wts = sb("wts", [EXPERTS, TOK])
        mbc = sb("mbc", [P, EXPERTS // EPQ, TOK])

        bank = [stack.enter_context(nc.psum_tensor(f"bank{i}", [P, 512], F32)) for i in range(8)]

        x_loaded = sem("x_loaded")
        v_loaded = sem("v_loaded")
        c_loaded = sem("c_loaded")
        w_const = sem("w_const")
        setup = sem("setup")
        neg_ready = sem("neg_ready")
        tanh_ready = sem("tanh_ready")
        sdt_ready = sem("sdt_ready")
        stored = sem("stored")
        N_CONST = 13

        block = stack.enter_context(nc.Block())

        @block.sync
        def _(sp):
            sp.dma_start(x[:], x_in.rearrange("(t p) d -> p t d", p=P)).then_inc(x_loaded, 16)
            consts = [(ident[:], ident_in),
                      (tg[:, 0:2], g_xattn.rearrange("(a n) -> a n", a=1).to_broadcast([P, 2])),
                      (tg[:, 2:4], g_ffn.rearrange("(a n) -> a n", a=1).to_broadcast([P, 2])),
                      (sg[:], s_gate), (su[:], s_up), (sd[:], s_down),
                      (wc[:], wc_t.rearrange("(k p) n -> p k n", p=P)),
                      (bcr[:], bc.rearrange("(a n) -> a n", a=1)),
                      (gw[:], gate_t.rearrange("(k p) n -> p k n", p=P))]
            for dst, src in consts[:3]:
                sp.dma_start(dst, src).then_inc(c_loaded, 16)
            for a in A:
                sp.wait_ge(a.k_zeroed, 1)
                for half, h in [(half, h) for half in range(2) for h in range(a.hk)]:
                    sp.dma_start(a.kbd[64 * half + h * a.d:64 * half + (h + 1) * a.d, :, h * KEYS:(h + 1) * KEYS],
                                 ctx_t[h * a.d:(h + 1) * a.d, :].rearrange("p (b t) -> p b t", t=KEYS)
                                 ).then_inc(a.k_loaded, 16)
                if a.layer == 0:
                    for half in range(2):
                        sp.dma_start(ctx_v[64 * half:64 * half + 64], ctx_in.rearrange("b t d -> t b d")
                                     ).then_inc(v_loaded, 16)
                    for dst, src in consts[3:]:
                        sp.dma_start(dst, src).then_inc(w_const, 16)

            def stream(m, raw, dram):
                def chunk(i, cc, first):
                    c = i * m.per_body + cc
                    if not (first and cc < 2):
                        sp.wait_ge(m.w_split, c - 1)
                    sp.dma_start(raw[:, cc % 2, :], dram[bass.ds(c, 1)].rearrange("a p n -> (a p) n")
                                 ).then_inc(m.w_loaded[cc % 2], 16)
                for cc in range(m.per_body):
                    chunk(0, cc, True)
                if m.chunks > m.per_body:
                    with sp.Fori(1, m.chunks // m.per_body) as i:
                        for cc in range(m.per_body):
                            chunk(i, cc, False)

            if stages > 1:
                stream(M[0], wrawi, w0)
            if stages > 3:
                sp.wait_ge(M[0].w_split, FFN_CHUNKS)
                stream(M[1], wraw, w1)
            out_v = out.rearrange("(t p) d -> p t d", p=P)
            last = A[0] if stages == 1 else M[0] if stages == 2 else A[1] if stages == 3 else M[1]
            for t in range(TT):
                sp.wait_ge(last.x_done, t + 1)
                sp.dma_start(out_v[:, t, :], x[:, t, :]).then_inc(stored, 16)
            sp.wait_ge(stored, 16 * TT)

        @block.gpsimd
        def _(pool):
            nc.gpsimd.memset(A[0].kbd[:], 0.0).then_inc(A[0].k_zeroed, 1)
            nc.gpsimd.memset(neghalf[:], -0.5).then_inc(neg_ready, 1)
            nc.gpsimd.memset(A[1].kbd[:], 0.0).then_inc(A[1].k_zeroed, 1)

            def power(m):
                pool.wait_ge(neg_ready, 1)
                pool.wait_ge(m.var_ready, 1)
                nc.gpsimd.tensor_tensor(rstd[:], ve[:], neghalf[:], ALU.pow).then_inc(m.rstd_ready, 1)

            def attention(a):
                power(a)
                if a.layer == 0:
                    with pool.Fori(0, TT) as t:
                        pool.wait_ge(a.y_done, UNITS * (t + 1))
                        nc.gpsimd.tensor_tensor(x[:, t, :], x[:, t, :], yt[:], ALU.add).then_inc(a.x_done, 1)

            def feed_forward(m):
                power(m)

                def body(i, first):
                    for cc in range(m.per_body):
                        c = i * m.per_body + cc
                        if m.layer == 0:
                            pool.wait_ge(m.w_loaded[cc % 2], 16 * (cc // 2 + 1))
                            if cc >= 2:
                                pool.wait_ge(m.w_split, c - 1)
                            nc.gpsimd.tensor_scalar(wf[:, cc % 2, :], wrawi[:, cc % 2, :], -ZERO_POINT, None,
                                                    ALU.add).then_inc(m.wf_ready, 1)
                        src = wf if m.layer == 0 else wraw
                        pool.wait_ge(m.wh_ready, c + 1)
                        nc.gpsimd.tensor_tensor(wl[:, cc % WRING, :], src[:, cc % 2, :],
                                                wh[:, cc % WRING, :].bitcast(F32), ALU.subtract
                                                ).then_inc(m.w_split, 1)
                body(0, True)
                if m.chunks > m.per_body:
                    with pool.Fori(1, m.chunks // m.per_body) as i:
                        body(i, False)

            attention(A[0])
            if stages > 1:
                feed_forward(M[0])
            if stages > 2:
                attention(A[1])
            if stages > 3:
                feed_forward(M[1])

        @block.scalar
        def _(act):
            act.wait_ge(c_loaded, 48)
            nc.scalar.activation(tg[:], tg[:], ACT.Tanh).then_inc(tanh_ready, 1)

            def attention(a):
                def q_copy(t):
                    act.wait_ge(a.q_transposed, t + 1)
                    for g2 in range(2):
                        p = slice(64 * g2, 64 * g2 + 64)
                        last = nc.scalar.activation(
                            qt[p, :, :, g2, :], bank[6][p, 0:DM].rearrange("p (c b s) -> p b c s", c=2, b=2), ACT.Copy)
                    last.then_inc(a.q_ready, 1)

                def exp(n, k, fresh):
                    act.wait_ge(a.sub_done, n + 1)
                    if not fresh:
                        act.wait_ge(a.pt_done, n - 1)
                    nc.scalar.activation(pt[:, k, 0:a.ns], dt_[:, k, 0:a.ns], ACT.Exp, scale=a.scale
                                         ).then_inc(a.p_ready, 1)

                def pt_copy(n, k, fresh):
                    act.wait_ge(a.pt_done, n + 1)
                    if not fresh:
                        act.wait_ge(a.av_done, n - 1)
                    nc.scalar.activation(pts[:, k, 0:a.npair, :],
                                         bank[2 + k][:, 0:a.ns].rearrange("p (j c) -> p j c", c=P), ACT.Copy
                                         ).then_inc(a.pts_ready, 1)

                def yt_copy(t):
                    act.wait_ge(a.yt_done, t + 1)
                    if not (isinstance(t, int) and t == 0):
                        act.wait_ge(a.proj_done, t)
                    nc.scalar.activation(yts[:], bank[7][:, 0:DM].rearrange("p (k c) -> p k c", c=P), ACT.Copy
                                         ).then_inc(a.yts_ready, 1)

                def tile(t, first, last):
                    for u in range(UNITS):
                        n = UNITS * t + u
                        exp(n, u % 2, first and u < 2)
                        if u == 1 and not last:
                            q_copy(t + 1)
                        if a.layer == 1 and not first and u == 2:
                            yt_copy(t - 1)
                        if not (first and u == 0):
                            pt_copy(n - 1, (u + 1) % 2, first and u < 3)

                act.wait_ge(setup, 2)
                q_copy(0)
                tile(0, True, False)
                with act.Fori(1, TT - 1) as t:
                    tile(t, False, False)
                tile(TT - 1, False, True)
                pt_copy(UNITS * TT - 1, 1, False)
                if a.layer == 1:
                    yt_copy(TT - 1)

            def feed_forward(m):
                def xt_copy(t, fresh):
                    act.wait_ge(m.xt_done, t + 1)
                    if not fresh:
                        act.wait_ge(m.xt_split, t)
                        if m.layer == 1:
                            act.wait_ge(m.logits_done, t)
                    nc.scalar.activation(xtf[:], bank[0][:, 0:DM].rearrange("p (k c) -> p k c", c=P), ACT.Copy
                                         ).then_inc(m.xtf_ready, 1)
                xt_copy(0, True)
                with act.Fori(1, TT) as t:
                    xt_copy(t, False)
                if m.layer == 0:
                    act.wait_ge(w_const, 16 * 6)
                else:
                    act.wait_ge(m.d_ready, 1)
                    nc.scalar.activation(ew[:], ew[:], ACT.Exp).then_inc(m.e_ready, 1)
                    act.wait_ge(m.wt_done, 1)
                    for k in range(2):
                        nc.scalar.activation(wts[:, k * BLK:(k + 1) * BLK], bank[2 + k][0:EXPERTS, :], ACT.Copy
                                             ).then_inc(m.wts_ready, 1)
                    act.wait_ge(m.wts_ready, 2)
                    act.dma_start(mask_dram, wts[:]).then_inc(m.w_stored, 16)
                    act.wait_ge(m.w_stored, 16)
                    src = mask_dram.rearrange("(q j) t -> j q t", j=EPQ)
                    for j in range(EPQ):
                        act.dma_start(mbc[32 * j:32 * j + 32],
                                      src[j:j + 1].to_broadcast([32, EXPERTS // EPQ, TOK])).then_inc(m.m_loaded, 16)

                def w_round(c, cc, i, fresh):
                    if m.layer == 0:
                        act.wait_ge(m.wf_ready, c + 1)
                    else:
                        act.wait_ge(m.w_loaded[cc % 2], 16 * (i * (m.per_body // 2) + cc // 2 + 1))
                    if not fresh:
                        act.wait_ge(m.dn_done, NBLK * (c - WRING + 1))
                    src = wf if m.layer == 0 else wraw
                    nc.scalar.activation(wh[:, cc % WRING, :], src[:, cc % 2, :], ACT.Copy).then_inc(m.wh_ready, 1)

                def body(i, first, last):
                    for cc in range(m.per_body):
                        c = i * m.per_body + cc
                        for k in range(NBLK):
                            n = NBLK * c + k
                            fresh = first and cc == 0
                            act.wait_ge(m.g_done, n + 1)
                            if not fresh:
                                act.wait_ge(m.t_done, n - 1)
                            scale = sg[:, c:c + 1] if m.layer == 0 else 1.0
                            nc.scalar.activation(s_t[:, k, :], bank[k][:], ACT.Silu, scale=scale
                                                 ).then_inc(m.s_ready, 1)
                            if k == 0 and not (last and cc == m.per_body - 1):
                                w_round(c + 1, (cc + 1) % m.per_body, i + (cc + 1) // m.per_body,
                                        first and cc + 1 < WRING)
                            act.wait_ge(m.h_full, n + 1)
                            if not fresh:
                                act.wait_ge(m.dn_done, n - 1)
                            nc.scalar.activation(hh[:, k, :], h_t[:, k, :], ACT.Copy).then_inc(m.hh_ready, 1)
                w_round(0, 0, 0, True)
                bodies = m.chunks // m.per_body
                body(0, True, bodies == 1)
                if bodies > 1:
                    with act.Fori(1, bodies - 1) as i:
                        body(i, False, False)
                    body(bodies - 1, False, True)
                if m.layer == 0:
                    act.wait_ge(sdt_ready, 1)
                act.wait_ge(m.dn_done, NBLK * m.chunks)
                for k in range(NBLK):
                    for h in range(KC):
                        scale = sdt[:, h:h + 1] if m.layer == 0 else tg[:, 3:4]
                        nc.scalar.activation(ot[:, h, k * BLK:(k + 1) * BLK], bank[4 + 2 * h + k][:], ACT.Copy,
                                             scale=scale).then_inc(m.ot_ready, 1)

            attention(A[0])
            if stages > 1:
                feed_forward(M[0])
            if stages > 2:
                attention(A[1])
            if stages > 3:
                feed_forward(M[1])

        @block.vector
        def _(dve):
            nc.vector.memset(ones[:], 1.0).then_inc(setup, 1)
            nc.vector.memset(qt[:], 0.0).then_inc(setup, 1)
            for a in A:
                nc.vector.memset(a.vbd[:], 0.0).then_inc(a.v_ready, 1)
                dve.wait_ge(a.v_ready, 1)
                nc.vector.memset(a.vbd[0:64, :, :, 2 * a.d:2 * a.d + 1], 1.0).then_inc(a.v_ready, 1)
                nc.vector.memset(a.vbd[64:128, :, :, 2 * a.d + 1:2 * a.d + 2], 1.0).then_inc(a.v_ready, 1)
            dve.wait_ge(v_loaded, 32)
            for a in A:
                for half in range(2):
                    p = slice(64 * half, 64 * half + 64)
                    src = ctx_v[p].rearrange("p b (j h d) -> p b j h d", h=2, d=a.d)[:, :, :, half, :]
                    nc.vector.tensor_copy(a.vbd[p, :, :, a.d * half:a.d * half + a.d], src).then_inc(a.v_ready, 1)

            def ln_stats(m, chain, before):
                for t in range(TT):
                    if before is not None:
                        dve.wait_ge(before.x_done, t + 1)
                    last = nc.vector.bn_stats(stats[:, t, :], x[:, t, :])
                chain.link(last)
                for t in range(TT):
                    last = nc.vector.bn_aggr(mv[:, t, :], stats[:, t, :])
                chain.link(last)
                nc.vector.tensor_scalar(ve[:].unsqueeze(2), mv[:, :, 1:2], EPS, None, ALU.add
                                        ).then_inc(m.var_ready, 1)
                dve.wait_ge(m.rstd_ready, 1)

            def ln_apply(m, t, dst, src):
                nc.vector.tensor_scalar(dst, src, mv[:, t, 0:1], rstd[:, bass.ds(t, 1)], ALU.subtract, ALU.mult
                                        ).then_inc(m.xn_ready, 1)

            def attention(a, before):
                chain = Chain(dve, a.dve_chain)

                def layer_norm(t, fresh):
                    if not fresh:
                        dve.wait_ge(a.q_transposed, t)
                    ln_apply(a, t, xn[:].rearrange("p (g h d) -> p h g d", g=G, d=a.d),
                             x[:, t, :].rearrange("p (h g d) -> p h g d", g=G, d=a.d))

                def softmax_max(n, k, fresh):
                    dve.wait_ge(a.scored, n + 1)
                    s = bank[k][:, 0:a.ns].rearrange("p (h t) -> p h t", t=KEYS)
                    chain.link(nc.vector.reduce_max(mx[:, k, 0:a.hk], s, AX.X))
                    if not fresh:
                        dve.wait_ge(a.p_ready, n - 1)
                    nc.vector.tensor_tensor(dt_[:, k, 0:a.ns].rearrange("p (h t) -> p h t", t=KEYS), s,
                                            mx[:, k, 0:a.hk].unsqueeze(2).to_broadcast([P, a.hk, KEYS]),
                                            ALU.subtract).then_inc(a.sub_done, 1)

                def normalise(n, t, u, fresh):
                    k, b2, gp = u % 2, u // 2, u % 2
                    o = bank[4 + k][:, 0:a.npair * a.vw].rearrange("p (j c) -> p j c", c=a.vw)
                    dve.wait_ge(a.av_done, n + 1)
                    chain.link(nc.vector.reciprocal(rc[:, k, 0:a.hk].rearrange("p (j h) -> p j h", h=2),
                                                    o[:, :, 2 * a.d:]))
                    if u == 0 and not fresh:
                        dve.wait_ge(a.x_done if a.layer == 0 else a.yt_done, t)
                    for g2 in range(2):
                        pi, po = slice(64 * g2, 64 * g2 + 64), slice(64 * b2, 64 * b2 + 64)
                        src = o[pi, :, 0:2 * a.d].rearrange("p j (h d) -> p j h d", h=2)
                        dst = yt[po].rearrange("p (j h g d) -> p j h g d", j=a.npair, h=2, g=G)[:, :, :, 2 * gp + g2, :]
                        r = rc[pi, k, 0:a.hk].rearrange("p (j h) -> p j h", h=2).unsqueeze(3).to_broadcast(
                            [64, a.npair, 2, a.d])
                        if a.layer == 0:
                            last = nc.vector.scalar_tensor_tensor(dst, src, tg[pi, 0:1], r, ALU.mult, ALU.mult)
                        else:
                            last = nc.vector.tensor_tensor(dst, src, r, ALU.mult)
                    last.then_inc(a.y_done, 1)

                def residual(t):
                    dve.wait_ge(a.proj_done, t + 1)
                    nc.vector.scalar_tensor_tensor(x[:, t, :], bank[7][:, 256:512], tg[:, 1:2], x[:, t, :],
                                                   ALU.mult, ALU.add).then_inc(a.x_done, 1)

                def tile(t, first, last):
                    for u in range(UNITS):
                        n = UNITS * t + u
                        softmax_max(n, u % 2, first and u < 2)
                        if u == 0 and not last:
                            layer_norm(t + 1, False)
                        if not (first and u < 2):
                            tn = t if u >= 2 else t - 1
                            normalise(n - 2, tn, (u + 2) % 4, first)
                        if a.layer == 1 and not first and u == 3:
                            residual(t - 1)

                ln_stats(a, chain, before)
                layer_norm(0, True)
                tile(0, True, False)
                links = 2 * UNITS
                base0 = chain.n
                with dve.Fori(1, TT - 1) as t:
                    chain.at((t - 1) * links + base0)
                    tile(t, False, False)
                    assert chain.n == links
                chain.at((TT - 2) * links + base0)
                tile(TT - 1, False, True)
                for n in (UNITS * TT - 2, UNITS * TT - 1):
                    normalise(n, TT - 1, n % 4, False)
                if a.layer == 1:
                    residual(TT - 1)

            def feed_forward(m, before):
                chain = Chain(dve, m.dve_chain)

                def layer_norm(t, fresh):
                    if not fresh:
                        dve.wait_ge(m.xt_done, t)
                    ln_apply(m, t, xn[:], x[:, t, :])

                def split(t):
                    tok = bass.ds(t * P, P)
                    dve.wait_ge(m.xtf_ready, t + 1)
                    chain.link(nc.vector.tensor_copy(xh[:, :, tok], xtf[:]))
                    nc.vector.tensor_tensor(xl[:, :, tok], xtf[:], xh[:, :, tok].bitcast(F32), ALU.subtract
                                            ).then_inc(m.xt_split, 1)
                ln_stats(m, chain, before)
                layer_norm(0, True)
                base0 = chain.n
                with dve.Fori(0, TT - 1) as t:
                    chain.at(base0 + t)
                    layer_norm(t + 1, False)
                    split(t)
                chain.at(base0 + (TT - 1))
                split(TT - 1)
                chain.at(base0 + (TT - 1) + 1)

                if m.layer == 0:
                    dve.wait_ge(w_const, 16 * 6)
                    dve.wait_ge(tanh_ready, 1)
                    nc.vector.tensor_scalar(sdt[:], sd[:], tg[:, 2:3], None, ALU.mult).then_inc(sdt_ready, 1)
                else:
                    dve.wait_ge(m.logits_done, TT)
                    chain.link(nc.vector.tensor_copy(lg[:], bank[1][:, 0:TT * EXPERTS].rearrange(
                        "p (t e) -> p t e", e=EXPERTS)))
                    for t in range(TT):
                        last = nc.vector.max(top[:, t, :], lg[:, t, :])
                    chain.link(last)
                    for t in range(TT):
                        last = nc.vector.match_replace(rep[:, t, :], top[:, t, :], lg[:, t, :], NEG)
                    chain.link(last)
                    nc.vector.tensor_tensor(ew[:], lg[:], top[:, :, 0:1].to_broadcast([P, TT, EXPERTS]),
                                            ALU.subtract).then_inc(m.d_ready, 1)
                    chain.link(nc.vector.tensor_tensor(rep[:], rep[:], lg[:], ALU.not_equal))
                    dve.wait_ge(m.e_ready, 1)
                    chain.link(nc.vector.tensor_tensor(ew[:], ew[:], rep[:], ALU.mult))
                    chain.link(nc.vector.reduce_sum(esum[:], ew[:], AX.X))
                    chain.link(nc.vector.reciprocal(esum[:], esum[:]))
                    nc.vector.tensor_tensor(ew[:], ew[:], esum[:].unsqueeze(2).to_broadcast([P, TT, EXPERTS]),
                                            ALU.mult).then_inc(m.w_ready, 1)

                def body(i, first):
                    for cc in range(m.per_body):
                        c = i * m.per_body + cc
                        for k in range(NBLK):
                            n = NBLK * c + k
                            dve.wait_ge(m.s_ready, n + 1)
                            dve.wait_ge(m.u_done, n + 1)
                            if m.layer == 0:
                                nc.vector.scalar_tensor_tensor(h_t[:, k, :], bank[2 + k][:], su[:, c:c + 1],
                                                               s_t[:, k, :], ALU.mult, ALU.mult
                                                               ).then_inc(m.t_done, 1)
                                dve.wait_ge(m.t_done, n + 1)
                            else:
                                nc.vector.tensor_tensor(t_t[:], bank[2 + k][:], s_t[:, k, :], ALU.mult
                                                        ).then_inc(m.t_done, 1)
                                dve.wait_ge(m.t_done, n + 1)
                                if first and cc == 0 and k == 0:
                                    dve.wait_ge(m.m_loaded, 16 * EPQ)
                                q = i * (m.per_body // CPQ) + cc // CPQ
                                nc.vector.tensor_tensor(h_t[:, k, :], t_t[:], mbc[:, q, k * BLK:(k + 1) * BLK],
                                                        ALU.mult).then_inc(m.h_full, 1)
                            dve.wait_ge(m.hh_ready, n + 1)
                            nc.vector.tensor_tensor(hl[:, k, :], h_t[:, k, :], hh[:, k, :].bitcast(F32),
                                                    ALU.subtract).then_inc(m.h_split, 1)
                body(0, True)
                if m.chunks > m.per_body:
                    with dve.Fori(1, m.chunks // m.per_body) as i:
                        body(i, False)
                for t in range(TT):
                    dve.wait_ge(m.back_done, t + 1)
                    nc.vector.tensor_tensor(x[:, t, :], bank[t % 2][:, 0:DM], x[:, t, :], ALU.add
                                            ).then_inc(m.x_done, 1)

            dve.wait_ge(x_loaded, 16)
            dve.wait_ge(tanh_ready, 1)
            attention(A[0], None)
            if stages > 1:
                feed_forward(M[0], A[0])
            if stages > 2:
                attention(A[1], M[0])
            if stages > 3:
                feed_forward(M[1], A[1])

        @block.tensor
        def _(pe):
            def attention(a, before):
                def q_transposes(t, fresh):
                    pe.wait_ge(a.xn_ready, t + 1)
                    if not fresh:
                        pe.wait_ge(a.q_ready, t)
                    for gp in range(G // 2):
                        last = nc.tensor.transpose(bank[6][:, gp * P:(gp + 1) * P], xn[:, gp * P:(gp + 1) * P], ident[:])
                    last.then_inc(a.q_transposed, 1)

                def scores(n, t, u, fresh):
                    pe.wait_ge(a.k_loaded, 32 * a.hk)
                    if u == 0:
                        pe.wait_ge(a.q_ready, t + 1)
                    if not fresh:
                        pe.wait_ge(a.sub_done, n - 1)
                    b2, gp = u // 2, u % 2
                    nc.tensor.matmul(bank[u % 2][:, 0:a.ns], qt[:, b2, gp, :, :],
                                     a.kbd[:, 2 * t + b2, :], start=True, stop=True).then_inc(a.scored, 1)

                def p_transposes(n, k, fresh):
                    pe.wait_ge(a.p_ready, n + 1)
                    if not fresh:
                        pe.wait_ge(a.pts_ready, n - 1)
                    for j in range(a.npair):
                        last = nc.tensor.transpose(bank[2 + k][:, j * P:(j + 1) * P], pt[:, k, j * P:(j + 1) * P],
                                                   ident[:])
                    last.then_inc(a.pt_done, 1)

                def values(n, t, u, fresh):
                    k = u % 2
                    pe.wait_ge(a.pts_ready, n + 1)
                    if not fresh:
                        pe.wait_ge(a.y_done, n - 1)
                    for j in range(a.npair):
                        last = nc.tensor.matmul(bank[4 + k][:, j * a.vw:(j + 1) * a.vw], pts[:, k, j, :],
                                                a.vbd[:, 2 * t + u // 2, j, :], start=True, stop=True)
                    last.then_inc(a.av_done, 1)

                def y_transposes(t, fresh):
                    pe.wait_ge(a.y_done, UNITS * (t + 1))
                    if not fresh:
                        pe.wait_ge(a.x_done, t)
                    for k in range(KC):
                        last = nc.tensor.transpose(bank[7][:, k * P:(k + 1) * P], yt[:, k * P:(k + 1) * P], ident[:])
                    last.then_inc(a.yt_done, 1)

                def project(t):
                    pe.wait_ge(a.yts_ready, t + 1)
                    o = bank[7][:, 256:512]
                    for k in range(KC):
                        nc.tensor.matmul(o, yts[:, k, :], wc[:, k, :], start=(k == 0), stop=False)
                    nc.tensor.matmul(o, ones[:], bcr[:], start=False, stop=True).then_inc(a.proj_done, 1)

                def tile(t, first, last):
                    for u in range(UNITS):
                        n = UNITS * t + u
                        if not (last and u >= 2):
                            scores(n + 2, t if u < 2 else t + 1, (u + 2) % 4, False)
                        if u == 1 and not last:
                            q_transposes(t + 1, False)
                        if a.layer == 1 and not first:
                            if u == 2:
                                y_transposes(t - 1, isinstance(t, int) and t == 1)
                            if u == 3:
                                project(t - 1)
                        p_transposes(n, u % 2, first and u < 2)
                        if not (first and u == 0):
                            values(n - 1, t if u > 0 else t - 1, (u + 3) % 4, first and u < 3)

                q_transposes(0, True)
                pe.wait_ge(a.v_ready, 5)
                scores(0, 0, 0, True)
                scores(1, 0, 1, True)
                tile(0, True, False)
                with pe.Fori(1, TT - 1) as t:
                    tile(t, False, False)
                tile(TT - 1, False, True)
                values(UNITS * TT - 1, TT - 1, 3, False)
                if a.layer == 1:
                    y_transposes(TT - 1, False)
                    project(TT - 1)

            def feed_forward(m):
                def x_transposes(t, fresh):
                    pe.wait_ge(m.xn_ready, t + 1)
                    if not fresh:
                        pe.wait_ge(m.xtf_ready, t)
                    for k in range(KC):
                        last = nc.tensor.transpose(bank[0][:, k * P:(k + 1) * P], xn[:, k * P:(k + 1) * P], ident[:])
                    last.then_inc(m.xt_done, 1)

                def router(t):
                    pe.wait_ge(m.xtf_ready, t + 1)
                    for k in range(KC):
                        last = nc.tensor.matmul(bank[1][:, bass.ds(t * EXPERTS, EXPERTS)], xtf[:, k, :], gw[:, k, :],
                                                start=(k == 0), stop=(k == KC - 1))
                    last.then_inc(m.logits_done, 1)

                x_transposes(0, True)
                if m.layer == 1:
                    router(0)
                with pe.Fori(1, TT) as t:
                    x_transposes(t, False)
                    if m.layer == 1:
                        router(t)
                if m.layer == 1:
                    pe.wait_ge(m.w_ready, 1)
                    for t in range(TT):
                        last = nc.tensor.transpose(bank[2 + t // 4][0:EXPERTS, (t % 4) * P:(t % 4 + 1) * P],
                                                   ew[:, t, :], ident[:])
                    last.then_inc(m.wt_done, 1)
                    pe.wait_ge(m.wts_ready, 2)
                pe.wait_ge(m.xt_split, TT)

                def product(o, w_sl, s, rh, rl, first, last, reopened=False):
                    nc.tensor.matmul(o, wh[:, s, w_sl], rh, start=first, stop=False, skip_group_check=reopened)
                    nc.tensor.matmul(o, wh[:, s, w_sl], rl, start=False, stop=False, skip_group_check=reopened)
                    return nc.tensor.matmul(o, wl[:, s, w_sl], rh, start=False, stop=last, skip_group_check=reopened)

                def gate_up(n, c, s, k, fresh):
                    if k == 0:
                        pe.wait_ge(m.w_split, c + 1)
                    tok = slice(k * BLK, (k + 1) * BLK)
                    for col, bk, free, done in ((0, k, m.s_ready, m.g_done), (DM, 2 + k, m.t_done, m.u_done)):
                        if not fresh:
                            pe.wait_ge(free, n - 1)
                        for h in range(KC):
                            last = product(bank[bk][:], slice(col + h * P, col + (h + 1) * P), s, xh[:, h, tok],
                                           xl[:, h, tok], h == 0, h == KC - 1)
                        last.then_inc(done, 1)

                def down(n, s, k, first):
                    pe.wait_ge(m.h_split, n + 1)
                    for h in range(KC):
                        ins = product(bank[4 + 2 * h + k][:], slice(2 * DM + h * P, 2 * DM + (h + 1) * P), s,
                                      hh[:, k, :], hl[:, k, :], first, True, reopened=True)
                    ins.then_inc(m.dn_done, 1)

                def body(i, first):
                    for cc in range(m.per_body):
                        c = i * m.per_body + cc
                        for k in range(NBLK):
                            n = NBLK * c + k
                            gate_up(n, c, cc % WRING, k, first and cc == 0)
                            if not (first and n == 0):
                                down(n - 1, (cc if k else cc - 1) % WRING, 1 - k, first and n <= 2)
                body(0, True)
                if m.chunks > m.per_body:
                    with pe.Fori(1, m.chunks // m.per_body) as i:
                        body(i, False)
                down(NBLK * m.chunks - 1, (m.chunks - 1) % WRING, 1, False)
                for t in range(TT):
                    pe.wait_ge(m.ot_ready, 2 * (t // 4 + 1))
                    if t >= 2:
                        pe.wait_ge(m.x_done, t - 1)
                    for h in range(KC):
                        last = nc.tensor.transpose(bank[t % 2][:, h * P:(h + 1) * P], ot[:, h, t * P:(t + 1) * P],
                                                   ident[:])
                    last.then_inc(m.back_done, 1)

            pe.wait_ge(c_loaded, 16 * 3)
            pe.wait_ge(setup, 2)
            attention(A[0], None)
            pe.wait_ge(w_const, 16 * 6)
            if stages > 1:
                pe.wait_ge(A[0].y_done, UNITS * TT)
                feed_forward(M[0])
            if stages > 2:
                attention(A[1], M[0])
            if stages > 3:
                pe.wait_ge(A[1].x_done, TT)
                feed_forward(M[1])


STAGES = 4


def kernel(x, ctx_512, g_xattn, g_ffn, L0_ffn_wq_gate, L0_ffn_s_gate, L0_ffn_wq_up, L0_ffn_s_up, L0_ffn_wq_down,
           L0_ffn_s_down, L1_xattn_Wc, L1_xattn_bc, L1_ffn_gate_w, L1_ffn_w_gate_proj, L1_ffn_w_up_proj,
           L1_ffn_w_down_proj):
    import numpy as np
    import concourse.bacc as bacc
    from concourse import mybir as mb
    from concourse.bass_utils import run_bass_kernel_spmd as run

    A = np.asarray

    def halves(rows, n):
        return rows.reshape(n, P, KC, P).transpose(0, 3, 2, 1).reshape(n, P, DM)

    pad = FFN_CHUNKS * P - HIDDEN
    gate0 = np.pad(A(L0_ffn_wq_gate), ((0, pad), (0, 0)))
    up0 = np.pad(A(L0_ffn_wq_up), ((0, pad), (0, 0)))
    down0 = np.pad(A(L0_ffn_wq_down).T, ((0, pad), (0, 0)))
    w0 = np.concatenate([halves(gate0, FFN_CHUNKS), halves(up0, FFN_CHUNKS), down0.reshape(FFN_CHUNKS, P, DM)], 2)
    s_gate = np.pad(A(L0_ffn_s_gate), (0, pad)).reshape(FFN_CHUNKS, P).T
    s_up = np.pad(A(L0_ffn_s_up), (0, pad)).reshape(FFN_CHUNKS, P).T

    def rows(w):
        return w.reshape(EXPERTS // EPQ, EPQ, CPQ, 32, DM).transpose(0, 2, 1, 3, 4).reshape(MOE_CHUNKS * P, DM)
    w1 = np.concatenate([halves(rows(A(L1_ffn_w_gate_proj)), MOE_CHUNKS), halves(rows(A(L1_ffn_w_up_proj)), MOE_CHUNKS),
                         rows(A(L1_ffn_w_down_proj).transpose(0, 2, 1)).reshape(MOE_CHUNKS, P, DM)], 2)
    ctx = A(ctx_512)
    ins = {
        "x_in": A(x).reshape(TOK, DM),
        "ctx_t": ctx.transpose(2, 0, 1).reshape(64, BATCH * KEYS),
        "ctx_in": ctx,
        "g_xattn": A(g_xattn),
        "g_ffn": A(g_ffn),
        "w0": w0,
        "s_gate": s_gate,
        "s_up": s_up,
        "s_down": A(L0_ffn_s_down).reshape(KC, P).T,
        "wc_t": A(L1_xattn_Wc).T,
        "bc": A(L1_xattn_bc),
        "gate_t": A(L1_ffn_gate_w).T,
        "w1": w1,
        "ident_in": np.eye(P, dtype=np.float32),
    }
    nc = bacc.Bacc("TRN2", target_bir_lowering=False, num_devices=1)
    arrays, args = {}, []
    for name, a in ins.items():
        a = np.ascontiguousarray(a)
        arrays[name] = a
        args.append(nc.dram_tensor(name, a.shape, mb.dt.from_np(a.dtype), kind="ExternalInput").ap())
    args.append(nc.dram_tensor("mask_dram", (EXPERTS, TOK), F32).ap())
    args.append(nc.dram_tensor("out", (TOK, DM), F32, kind="ExternalOutput").ap())
    build(nc, *args, stages=STAGES)
    r = run(nc, [arrays], core_ids=[0])
    return r.results[0]["out"].reshape(BATCH, SEQ, DM)
```

```python
from contextlib import ExitStack

import concourse.bass as bass
from concourse import mybir

ALU = mybir.AluOpType
ACT = mybir.ActivationFunctionType
AX = mybir.AxisListType
F32 = mybir.dt.float32
F32R = mybir.dt.float32r
I32 = mybir.dt.int32

P = 128
DM = 256
KC = DM // P
COLS = 512
TT = 8
TOK = TT * P
BATCH = 16
SEQ = 64
KEYS = 64
G = 4
BLK = 512
NBLK = TOK // BLK
EXPERTS = 32
INNER = 96
TOPK = 8
EPQ = 4
CPQ = EPQ * INNER // P
MOE_CHUNKS = EXPERTS * INNER // P
WPACK = 3 * DM
WRING = 3
EPS = 1e-5
ZERO_POINT = 128.0
HIDDEN = 704
FFN_CHUNKS = (HIDDEN + P - 1) // P
NEG = -3.0e38
W_EARLY = (TT - 2, TT - 1)
MASK_BANKS = (4, 7, 5, 6)
AHEAD = 2


def after(eng, sem, value):
    if not (isinstance(value, int) and value <= 0):
        eng.wait_ge(sem, value)


def live(t):
    return not isinstance(t, int) or 0 <= t < TT


def early(t):
    return isinstance(t, int) and t in W_EARLY


def up_to(value, most):
    return min(value, most) if isinstance(value, int) else value


def over_tiles(eng, lag, body):
    for t in range(lag):
        body(t)
    with eng.Fori(lag, TT - AHEAD) as t:
        body(t)
    for t in range(TT - AHEAD, TT + lag):
        body(t)


class Chain:

    def __init__(self, eng, sem):
        self.eng, self.sem, self.base, self.n = eng, sem, 0, 0

    def at(self, base):
        self.base, self.n = base, 0

    def mark(self, ins):
        ins.then_inc(self.sem, 1)
        self.n += 1

    def now(self):
        return self.base + self.n

    def wait(self, value=None):
        self.eng.wait_ge(self.sem, self.now() if value is None else value)

    def link(self, ins):
        self.mark(ins)
        self.wait()


class Attention:

    def __init__(self, layer, kv_heads, kbd, vbd, sb, sem):
        self.layer, self.hk = layer, kv_heads
        self.d = DM // G // kv_heads
        self.ns = kv_heads * KEYS
        self.npair = kv_heads // 2
        self.gpu = COLS // self.ns
        self.units = 2 * (G // 2) // self.gpu
        self.lag = 3 if layer == 0 else 4
        self.x_bank = 7 if layer == 0 else 6
        self.scale = float(self.d) ** -0.5
        n = f"a{layer}_"
        self.kbd = kbd[:, :, :].rearrange("p r (b n) -> p r b n", n=self.ns)
        self.vbd = vbd[:, 0:BATCH * self.npair * P].rearrange("p (b j c) -> p b j c", j=self.npair, c=P)
        self.kmask = sb(n + "kmask", [P, self.hk])
        self.k_ready = sem(n + "k_ready")
        self.v_ready = sem(n + "v_ready")
        self.var_ready = sem(n + "var_ready")
        self.rstd_ready = sem(n + "rstd_ready")
        self.xn_ready = sem(n + "xn_ready")
        self.qh_ready = sem(n + "qh_ready")
        self.q_split = sem(n + "q_split")
        self.q_transposed = sem(n + "q_transposed")
        self.q_ready = sem(n + "q_ready")
        self.scored = sem(n + "scored")
        self.sub_done = sem(n + "sub_done")
        self.p_ready = sem(n + "p_ready")
        self.pt_done = sem(n + "pt_done")
        self.pts_ready = sem(n + "pts_ready")
        self.av_done = sem(n + "av_done")
        self.y_done = sem(n + "y_done")
        self.x_done = sem(n + "x_done")
        self.xb_ready = sem(n + "xb_ready")
        self.yt_done = sem(n + "yt_done")
        self.yts_ready = sem(n + "yts_ready")
        self.proj_done = sem(n + "proj_done")
        self.dve_chain = sem(n + "dve_chain")

    def unit(self, u):
        return (u // 2, [u % 2]) if self.gpu == 1 else (u, [0, 1])


class Mlp:

    def __init__(self, layer, chunks, per_body, sem):
        self.layer, self.chunks, self.per_body = layer, chunks, per_body
        n = f"m{layer}_"
        self.var_ready = sem(n + "var_ready")
        self.rstd_ready = sem(n + "rstd_ready")
        self.xn_ready = sem(n + "xn_ready")
        self.xt_done = sem(n + "xt_done")
        self.xtf_ready = sem(n + "xtf_ready")
        self.xh_ready = sem(n + "xh_ready")
        self.xt_split = sem(n + "xt_split")
        self.wf_ready = sem(n + "wf_ready")
        self.wh_ready = sem(n + "wh_ready")
        self.w_split = sem(n + "w_split")
        self.g_done = sem(n + "g_done")
        self.u_done = sem(n + "u_done")
        self.s_ready = sem(n + "s_ready")
        self.t_done = sem(n + "t_done")
        self.h_full = self.t_done if layer == 0 else sem(n + "h_full")
        self.hh_ready = sem(n + "hh_ready")
        self.h_split = sem(n + "h_split")
        self.dn_done = sem(n + "dn_done")
        self.ot_ready = [sem(n + f"ot_ready{k}") for k in range(NBLK)]
        self.back_done = sem(n + "back_done")
        self.x_done = sem(n + "x_done")
        self.dve_chain = sem(n + "dve_chain")
        self.w_loaded = [sem(n + f"w_loaded{i}") for i in range(2)]


class Route:

    def __init__(self, sem):
        self.gw_split = sem("r_gw_split")
        self.logits_done = sem("r_logits_done")
        self.d_ready = sem("r_d_ready")
        self.e_ready = sem("r_e_ready")
        self.w_ready = sem("r_w_ready")
        self.wt_done = sem("r_wt_done")
        self.wt_hi = sem("r_wt_hi")
        self.wt_lo = sem("r_wt_lo")
        self.sel_loaded = sem("r_sel_loaded")
        self.sel_ready = sem("r_sel_ready")
        self.spread_done = sem("r_spread_done")
        self.mask_ready = [sem("r_mask_ready0"), sem("r_mask_ready1")]
        self.chain = sem("r_chain")


def build(nc, x_in, ctx_t, ctx_in, g_xattn, g_ffn, w0, s_gate, s_up, s_down, wc_t, bc, gate_t, w1, ident_in, kmask0, kmask1, sel_in,
          out):
    with ExitStack() as stack:
        def sb(name, shape, dt=F32):
            return stack.enter_context(nc.sbuf_tensor(name, shape, dt))

        def sem(name):
            return stack.enter_context(nc.semaphore(name))

        kbd0 = sb("kbd0", [P, 2, BATCH * 8 * KEYS], F32R)
        kbd1 = kbd0[:, 1].rearrange("p (r n) -> p r n", r=2)
        vbd = sb("vbd", [P, BATCH * 4 * P])
        A = [Attention(0, 8, kbd0, vbd, sb, sem), Attention(1, 4, kbd1, vbd, sb, sem)]
        R = Route(sem)
        M = [Mlp(0, FFN_CHUNKS, FFN_CHUNKS, sem), Mlp(1, MOE_CHUNKS, 2 * CPQ, sem)]

        x = sb("x", [P, TT, DM])
        ident = sb("ident", [P, P])
        ctx_k = sb("ctx_k", [P, BATCH, KEYS])
        kh = sb("kh", [P, BATCH, KEYS], F32R)
        kl = sb("kl", [P, BATCH, KEYS])
        ctx_v = sb("ctx_v", [P, BATCH, 64])
        tg = sb("tg", [P, 4])
        sg = sb("sg", [P, FFN_CHUNKS])
        su = sb("su", [P, FFN_CHUNKS])
        sd = sb("sd", [P, KC])
        sdt = sb("sdt", [P, KC])
        wc = sb("wc", [P, KC, DM])
        bcb = sb("bcb", [P, DM])
        gw = sb("gw", [P, KC, EXPERTS])
        gwh = sb("gwh", [P, KC, EXPERTS], F32R)
        gwl = sb("gwl", [P, KC, EXPERTS], F32R)
        stats = sb("stats", [P, TT, 6])
        mv = sb("mv", [P, TT, 2])
        ve = sb("ve", [P, TT])
        neghalf = sb("neghalf", [P, TT])
        one = sb("one", [P, 1])
        rstd = sb("rstd", [P, TT])
        xn = sb("xn", [P, DM])
        stats2 = sb("stats2", [P, 6])
        mv2 = sb("mv2", [P, 2])
        ve2 = sb("ve2", [P, 1])
        rstd2 = sb("rstd2", [P, 1])
        xm = sb("xm", [P, DM])
        xb = sb("xb", [P, DM])
        qs = sb("qs", [P, G, 2, 64], F32R)
        qt = sb("qt", [P, 2, G, SEQ], F32R)
        mx = sb("mx", [P, 2, 8])
        dt_pt = sb("dt_pt", [P, 2, 2, 512])
        dt_, pt = dt_pt[:, 0], dt_pt[:, 1]
        pts = sb("pts", [P, 2, 4, P])
        rc = sb("rc", [P, 2, 16])
        yt = sb("yt", [P, DM])
        yts = sb("yts", [P, KC, P])
        xtf = sb("xtf", [P, KC, P])
        xh = sb("xh", [P, KC, TOK], F32R)
        xl = sb("xl", [P, KC, TOK], F32R)
        wraw = sb("wraw", [P, 2, WPACK])
        wrawi = wraw[:].bitcast(I32)
        wf = sb("wf", [P, 2, WPACK])
        wh = sb("wh", [P, WRING, WPACK], F32R)
        wl = sb("wl", [P, WRING, WPACK], F32R)
        s_t = pts[:].rearrange("p k j c -> p k (j c)")
        t_t = sb("t_t", [P, BLK])
        h_t = sb("h_t", [P, 2, BLK])
        hh = sb("hh", [P, 2, BLK], F32R)
        hl = sb("hl", [P, 2, BLK], F32R)
        ot = dt_pt[:].rearrange("p a b n -> p a (b n)")
        top = sb("top", [P, TT, TOPK])
        esum = sb("esum", [P, TT])
        te = TT * EXPERTS
        free = vbd[:, BATCH * A[1].npair * P:]
        lg, rep, ew = (free[:, i * te:(i + 1) * te].rearrange("p (t e) -> p t e", e=EXPERTS) for i in range(3))
        sel_raw = free[0:2 * EXPERTS, TOK:2 * TOK]
        sel = kbd0[0:2 * EXPERTS, 0, 0:TOK]
        wts = kbd0[0:2 * EXPERTS, 0, TOK:2 * TOK]
        mbc = vbd[:].rearrange("p (q t) -> p q t", q=EXPERTS // EPQ)

        bank = [stack.enter_context(nc.psum_tensor(f"bank{i}", [P, 512], F32)) for i in range(8)]

        x_loaded = [sem("x_loaded0"), sem("x_loaded1")]
        k_loaded = sem("k_loaded")
        v_loaded = sem("v_loaded")
        c_loaded = sem("c_loaded")
        w_const = sem("w_const")
        neg_ready = sem("neg_ready")
        tanh_ready = sem("tanh_ready")
        kh_ready = sem("kh_ready")
        kl_ready = sem("kl_ready")
        k0_ready = sem("k0_ready")
        bcb_ready = sem("bcb_ready")
        sdt_ready = sem("sdt_ready")
        stored = sem("stored")

        block = stack.enter_context(nc.Block())

        def keys(ops, a, t, r, ready):
            b = bass.ds(2 * t, 2)
            shape = [P, 2, a.hk, KEYS]
            part = kh[:].bitcast(F32) if r == 0 else kl[:]
            ops.tensor_tensor(a.kbd[:, r, b, :].rearrange("p b (h t) -> p b h t", t=KEYS),
                              part[:, b, :].unsqueeze(2).to_broadcast(shape),
                              a.kmask[:].unsqueeze(1).unsqueeze(3).to_broadcast(shape), ALU.mult
                              ).then_inc(ready, 1)

        def value_pattern(eng, ops, a):
            ops.memset(a.vbd, 0.0).then_inc(a.v_ready, 1)
            for i in range(a.hk):
                half = slice(64 * (i % 2), 64 * (i % 2) + 64)
                eng.wait_ge(a.v_ready, i + 1)
                ops.memset(a.vbd[half, :, i // 2, 64 + i:65 + i], 1.0).then_inc(a.v_ready, 1)
            eng.wait_ge(a.v_ready, a.hk + 1)

        @block.sync
        def _(sp):
            x_v = x_in.rearrange("(t p) d -> p t d", p=P)
            sp.dma_start(x[:, 0:2, :], x_v[:, 0:2, :]).then_inc(x_loaded[0], 16)
            sp.dma_start(ident[:], ident_in).then_inc(c_loaded, 16)
            for half in range(2):
                sp.dma_start(ctx_k[64 * half:64 * half + 64], ctx_t.rearrange("p (b t) -> p b t", t=KEYS)
                             ).then_inc(k_loaded, 16)
            for a, src in zip(A, (kmask0, kmask1)):
                sp.dma_start(a.kmask[:], src).then_inc(k_loaded, 16)
            sp.dma_start(x[:, 2:TT, :], x_v[:, 2:TT, :]).then_inc(x_loaded[1], 16)
            for dst, src in ((tg[:, 0:2], g_xattn), (tg[:, 2:4], g_ffn)):
                sp.dma_start(dst, src.rearrange("(a n) -> a n", a=1).to_broadcast([P, 2])).then_inc(c_loaded, 16)
            for half in range(2):
                sp.dma_start(ctx_v[64 * half:64 * half + 64], ctx_in.rearrange("b t d -> t b d")
                             ).then_inc(v_loaded, 16)
            for dst, src in ((sg[:], s_gate), (su[:], s_up), (sd[:], s_down),
                             (wc[:], wc_t.rearrange("(k p) n -> p k n", p=P)),
                             (bcb[:], bc.rearrange("(a n) -> a n", a=1).to_broadcast([P, DM])),
                             (gw[:], gate_t.rearrange("(k p) n -> p k n", p=P))):
                sp.dma_start(dst, src).then_inc(w_const, 16)

            def stream(m, raw, dram):
                def chunk(i, cc, first):
                    c = i * m.per_body + cc
                    if not (first and cc < 2):
                        sp.wait_ge(m.wf_ready if m.layer == 0 else m.w_split, c - 1)
                    sp.dma_start(raw[:, cc % 2, :], dram[bass.ds(c, 1)].rearrange("a p n -> (a p) n")
                                 ).then_inc(m.w_loaded[cc % 2], 16)
                for cc in range(m.per_body):
                    chunk(0, cc, True)
                if m.chunks > m.per_body:
                    with sp.Fori(1, m.chunks // m.per_body) as i:
                        for cc in range(m.per_body):
                            chunk(i, cc, False)

            stream(M[0], wrawi, w0)
            sp.wait_ge(M[0].w_split, FFN_CHUNKS)
            sp.wait_ge(A[0].av_done, A[0].units * TT)
            sp.dma_start(sel_raw, sel_in).then_inc(R.sel_loaded, 16)
            stream(M[1], wraw, w1)
            out_v = out.rearrange("(t p) d -> p t d", p=P)
            for t in range(TT):
                sp.wait_ge(M[1].x_done, t + 1)
                sp.dma_start(out_v[:, t, :], x[:, t, :]).then_inc(stored, 16)
            sp.wait_ge(stored, 16 * TT)

        @block.gpsimd
        def _(pool):
            nc.gpsimd.memset(neghalf[:], -0.5).then_inc(neg_ready, 1)
            nc.gpsimd.memset(one[:], 1.0).then_inc(neg_ready, 1)

            def power(m, t, dst, src):
                pool.wait_ge(m.var_ready, t + 1)
                nc.gpsimd.tensor_tensor(dst, src, neghalf[:, 0:src.shape[-1]], ALU.pow).then_inc(m.rstd_ready, 1)

            def q_split(a, t):
                src = xn[:].rearrange("p (g d) -> p g d", g=G)
                pool.wait_ge(a.xn_ready, t + 1)
                after(pool, a.q_transposed, t)
                nc.gpsimd.tensor_tensor(qs[:, :, 0, :], src, one[:].unsqueeze(2).to_broadcast([P, G, 64]),
                                        ALU.mult).then_inc(a.qh_ready, 1)
                pool.wait_ge(a.qh_ready, t + 1)
                nc.gpsimd.tensor_tensor(qs[:, :, 1, :], src, qs[:, :, 0, :].bitcast(F32), ALU.subtract
                                        ).then_inc(a.q_split, 1)

            def w_lo(m, c, cc):
                src = wf if m.layer == 0 else wraw
                pool.wait_ge(m.wh_ready, c + 1)
                nc.gpsimd.tensor_tensor(wl[:, cc % WRING, :], src[:, cc % 2, :], wh[:, cc % WRING, :].bitcast(F32),
                                        ALU.subtract).then_inc(m.w_split, 1)

            def attention(a, m):
                def x_split(t):
                    tok = bass.ds(t * P, P)
                    pool.wait_ge(m.xtf_ready, t + 1)
                    nc.gpsimd.tensor_tensor(xh[:, :, tok], xtf[:], one[:].unsqueeze(2).to_broadcast([P, KC, P]),
                                            ALU.mult).then_inc(m.xh_ready, 1)
                    pool.wait_ge(m.xh_ready, t + 1)
                    nc.gpsimd.tensor_tensor(xl[:, :, tok], xtf[:], xh[:, :, tok].bitcast(F32), ALU.subtract
                                            ).then_inc(m.xt_split, 1)

                def add_output(t):
                    pool.wait_ge(a.y_done, 2 * (t + 1))
                    nc.gpsimd.tensor_tensor(x[:, t, :], x[:, t, :], yt[:], ALU.add).then_inc(a.x_done, 1)

                def add_bias(t):
                    after(pool, a.x_done, t)
                    nc.gpsimd.tensor_tensor(xb[:], x[:, t, :], bcb[:], ALU.add).then_inc(a.xb_ready, 1)

                def both_keys(t):
                    for r in range(2):
                        keys(nc.gpsimd, a, t, r, a.k_ready)

                def body(t):
                    tile_steps(t)
                    if early(t):
                        w_lo(m, W_EARLY.index(t), W_EARLY.index(t))

                def tile_steps(t):
                    if a.layer == 0:
                        if live(t - 2):
                            power(m, t - 2, rstd2[:], ve2[:])
                        if live(t - 3):
                            x_split(t - 3)
                        if live(t + 2):
                            both_keys(t + 2)
                        if live(t - 1):
                            add_output(t - 1)
                        if live(t + 2):
                            q_split(a, t + 2)
                    else:
                        if live(t - 2):
                            add_bias(t - 2)
                        if live(t + 2):
                            q_split(a, t + 2)
                        if live(t - 3):
                            x_split(t - 3)
                        if live(t - 2):
                            power(m, t - 2, rstd2[:], ve2[:])

                if a.layer == 0:
                    pool.wait_ge(kl_ready, 2)
                    both_keys(1)
                else:
                    pool.wait_ge(A[0].av_done, A[0].units * TT)
                    value_pattern(pool, nc.gpsimd, a)
                    for t in range(2):
                        both_keys(t)
                    with pool.Fori(2, TT) as t:
                        both_keys(t)
                    pool.wait_ge(bcb_ready, 1)
                    power(a, 0, rstd[:, 0:AHEAD], ve[:, 0:AHEAD])
                    q_split(a, 0)
                q_split(a, 1)
                power(a, 1, rstd[:, AHEAD:TT], ve[:, AHEAD:TT])
                over_tiles(pool, a.lag, body)

            def feed_forward(m):

                def body(i, first):
                    for cc in range(m.per_body):
                        if not (first and cc < len(W_EARLY)):
                            w_lo(m, i * m.per_body + cc, cc)
                body(0, True)
                if m.chunks > m.per_body:
                    with pool.Fori(1, m.chunks // m.per_body) as i:
                        body(i, False)

            value_pattern(pool, nc.gpsimd, A[0])
            pool.wait_ge(neg_ready, 2)
            pool.wait_ge(kh_ready, 1)
            for b in (slice(0, 2), slice(2, BATCH)):
                nc.gpsimd.tensor_tensor(kl[:, b], ctx_k[:, b], kh[:, b].bitcast(F32), ALU.subtract
                                        ).then_inc(kl_ready, 1)
                if b.start == 0:
                    power(A[0], 0, rstd[:, 0:AHEAD], ve[:, 0:AHEAD])
                    q_split(A[0], 0)
            attention(A[0], M[0])
            feed_forward(M[0])
            attention(A[1], M[1])
            feed_forward(M[1])

        @block.scalar
        def _(act):
            act.wait_ge(c_loaded, 48)
            nc.scalar.activation(tg[:], tg[:], ACT.Tanh).then_inc(tanh_ready, 1)
            act.wait_ge(k_loaded, 64)
            nc.scalar.activation(kh[:], ctx_k[:], ACT.Copy).then_inc(kh_ready, 1)
            act.wait_ge(tanh_ready, 1)
            act.wait_ge(v_loaded, 32)

            def w_hi(m, c, cc=None, i=0):
                cc = c if cc is None else cc
                act.wait_ge(m.w_loaded[cc % 2], 16 * (i * (m.per_body // 2) + cc // 2 + 1))
                src = wraw
                if m.layer == 0:
                    after(act, m.w_split, c - 1)
                    nc.scalar.activation(wf[:, cc % 2, :], wrawi[:, cc % 2, :], ACT.Copy, bias=-ZERO_POINT
                                         ).then_inc(m.wf_ready, 1)
                    act.wait_ge(m.wf_ready, c + 1)
                    src = wf
                after(act, m.dn_done, NBLK * (c - WRING + 1))
                nc.scalar.activation(wh[:, cc % WRING, :], src[:, cc % 2, :], ACT.Copy).then_inc(m.wh_ready, 1)

            def values(a):
                act.wait_ge(a.v_ready, a.hk + 1)
                for i in range(a.hk):
                    half = slice(64 * (i % 2), 64 * (i % 2) + 64)
                    cols = slice(i * a.d, (i + 1) * a.d)
                    scale = tg[half, 0:1] if a.layer == 0 else 1.0
                    nc.scalar.activation(a.vbd[half, :, i // 2, cols], ctx_v[half, :, cols], ACT.Copy, scale=scale
                                         ).then_inc(a.v_ready, 1)

            def attention(a, m):
                def q_copy(t):
                    act.wait_ge(a.q_transposed, t + 1)
                    after(act, a.scored, a.units * t)
                    nc.scalar.activation(qt[:], bank[6][:].rearrange("p (g b s) -> p b g s", b=2, s=SEQ), ACT.Copy
                                         ).then_inc(a.q_ready, 1)

                def exp(n, k):
                    act.wait_ge(a.sub_done, n + 1)
                    after(act, a.pt_done, n - 1)
                    nc.scalar.activation(pt[:, k, :], dt_[:, k, :], ACT.Exp, scale=a.scale).then_inc(a.p_ready, 1)

                def pt_copy(n, k):
                    act.wait_ge(a.pt_done, n + 1)
                    after(act, a.av_done, n - 1)
                    nc.scalar.activation(pts[:, k, :, :], bank[2 + k][:].rearrange("p (j c) -> p j c", c=P), ACT.Copy
                                         ).then_inc(a.pts_ready, 1)

                def yt_copy(t):
                    act.wait_ge(a.yt_done, t + 1)
                    after(act, a.proj_done, t)
                    nc.scalar.activation(yts[:], bank[7][:, 0:DM].rearrange("p (k c) -> p k c", c=P), ACT.Copy
                                         ).then_inc(a.yts_ready, 1)

                def xt_copy(t):
                    act.wait_ge(m.xt_done, t + 1)
                    after(act, m.xt_split, t)
                    nc.scalar.activation(xtf[:], bank[a.x_bank][:, 0:DM].rearrange("p (k c) -> p k c", c=P), ACT.Copy
                                         ).then_inc(m.xtf_ready, 1)

                def body(t):
                    for u in range(a.units):
                        n = a.units * t + u
                        if a.layer == 1 and u == 0 and live(t - 2):
                            yt_copy(t - 2)
                        if u == a.units - 2 and live(t + 1):
                            q_copy(t + 1)
                        if live(t if u else t - 1):
                            pt_copy(n - 1, (u + 1) % 2)
                        if live(t):
                            exp(n, u % 2)
                        if a.layer == 0 and u == 0 and live(t - 3):
                            xt_copy(t - 3)
                        if a.layer == 1 and u == 1 and live(t - 3):
                            xt_copy(t - 3)
                        if u == a.units // 2 and early(t):
                            w_hi(m, W_EARLY.index(t))

                q_copy(0)
                values(a)
                over_tiles(act, a.lag, body)

            def feed_forward(m):
                if m.layer == 0:
                    act.wait_ge(w_const, 16 * 6)

                def gate(n, c, k):
                    act.wait_ge(m.g_done, n + 1)
                    after(act, m.t_done, n - 1)
                    scale = sg[:, c:c + 1] if m.layer == 0 else 1.0
                    nc.scalar.activation(s_t[:, k, :], bank[k][:], ACT.Silu, scale=scale).then_inc(m.s_ready, 1)

                def route():
                    act.wait_ge(R.d_ready, 1)
                    nc.scalar.activation(ew, ew, ACT.Exp).then_inc(R.e_ready, 1)
                    for k in range(NBLK):
                        gate(k, 0, k)
                    act.wait_ge(R.wt_done, 1)
                    for k in range(NBLK):
                        nc.scalar.activation(wts[0:EXPERTS, k * BLK:(k + 1) * BLK], bank[5 + k][0:EXPERTS, :], ACT.Copy
                                             ).then_inc(R.wt_hi, 1)
                    for q in range(EXPERTS // EPQ):
                        act.wait_ge(R.spread_done, NBLK * q + 1)
                        nc.scalar.activation(mbc[:, q, 0:BLK], bank[MASK_BANKS[2 * q % 4]][:], ACT.Copy
                                             ).then_inc(R.mask_ready[0], 1)

                def body(i, first, last):
                    for cc in range(m.per_body):
                        c = i * m.per_body + cc
                        for k in range(NBLK):
                            n = NBLK * c + k
                            fresh = first and cc == 0
                            if not (fresh and m.layer == 1):
                                gate(n, c, k)
                            ready = first and cc + 1 < len(W_EARLY)
                            if k == 0 and not ready and not (last and cc == m.per_body - 1):
                                w_hi(m, c + 1, (cc + 1) % m.per_body, i + (cc + 1) // m.per_body)
                            act.wait_ge(m.h_full, n + 1)
                            if not fresh:
                                act.wait_ge(m.dn_done, n - 1)
                            nc.scalar.activation(hh[:, k, :], h_t[:, k, :], ACT.Copy).then_inc(m.hh_ready, 1)
                if m.layer == 1:
                    route()
                bodies = m.chunks // m.per_body
                body(0, True, bodies == 1)
                if bodies > 1:
                    with act.Fori(1, bodies - 1) as i:
                        body(i, False, False)
                    body(bodies - 1, False, True)
                if m.layer == 0:
                    act.wait_ge(sdt_ready, 1)
                act.wait_ge(m.dn_done, NBLK * m.chunks - 1)
                for h in range(KC):
                    scale = sdt[:, h:h + 1] if m.layer == 0 else tg[:, 3:4]
                    nc.scalar.activation(ot[:, h, 0:BLK], bank[4 + 2 * h][:], ACT.Copy, scale=scale
                                         ).then_inc(m.ot_ready[0], 1)

            attention(A[0], M[0])
            feed_forward(M[0])
            attention(A[1], M[1])
            feed_forward(M[1])

        @block.vector
        def _(dve):
            def ln_stats(m, chain, before, t0, t1):
                for t in range(t0, t1):
                    if before is not None:
                        dve.wait_ge(before.x_done, t + 1)
                    last = nc.vector.bn_stats(stats[:, t, :], x[:, t, :])
                chain.link(last)
                for t in range(t0, t1):
                    last = nc.vector.bn_aggr(mv[:, t, :], stats[:, t, :])
                chain.link(last)

            def attention(a, m, before):
                chain = Chain(dve, a.dve_chain)

                def layer_norm(t):
                    if isinstance(t, int) and t == AHEAD:
                        dve.wait_ge(a.rstd_ready, 2)
                    after(dve, a.q_split, t)
                    nc.vector.tensor_scalar(xn[:].rearrange("p (g h d) -> p h g d", g=G, d=a.d),
                                            x[:, t, :].rearrange("p (h g d) -> p h g d", g=G, d=a.d),
                                            mv[:, t, 0:1], rstd[:, bass.ds(t, 1)], ALU.subtract, ALU.mult
                                            ).then_inc(a.xn_ready, 1)

                def shift(n, k, between):
                    dve.wait_ge(a.scored, n + 1)
                    s = bank[k][:].rearrange("p (h t) -> p h t", t=KEYS)
                    chain.mark(nc.vector.reduce_max(mx[:, k, :], s, AX.X))
                    done = chain.now()
                    between()
                    chain.wait(done)
                    after(dve, a.p_ready, n - 1)
                    nc.vector.tensor_tensor(dt_[:, k, :].rearrange("p (h t) -> p h t", t=KEYS), s,
                                            mx[:, k, :].unsqueeze(2).to_broadcast([P, 8, KEYS]),
                                            ALU.subtract).then_inc(a.sub_done, 1)

                def normalise(t, b2, stats_of=None):
                    q = 2 * t + b2
                    if stats_of is not None:
                        next_wait(stats_of)
                    dve.wait_ge(a.av_done, a.units // 2 * (q + 1))
                    o = bank[4 + b2][:, 0:2 * P].rearrange("p (i c) -> p i c", c=P)
                    rs = rc[:, b2, 0:2 * a.hk].rearrange("p (i h) -> p i h", i=2)
                    chain.mark(nc.vector.reciprocal(rs, o[:, :, 64:64 + a.hk]))
                    if stats_of is not None:
                        next_stats(stats_of)
                    chain.wait()
                    if b2 == 0:
                        after(dve, a.x_done if a.layer == 0 else a.yt_done, t)
                    for g2 in range(2):
                        pi, po = slice(64 * g2, 64 * g2 + 64), slice(64 * b2, 64 * b2 + 64)
                        last = nc.vector.tensor_tensor(
                            yt[po].rearrange("p (h i g d) -> p i h g d", h=a.hk, i=2, g=2)[:, :, :, g2, :],
                            o[pi, :, 0:64].rearrange("p i (h d) -> p i h d", d=a.d),
                            rs[pi].unsqueeze(3).to_broadcast([64, 2, a.hk, a.d]), ALU.mult)
                    last.then_inc(a.y_done, 1)

                def residual(t):
                    dve.wait_ge(a.xb_ready, t + 1)
                    dve.wait_ge(a.proj_done, t + 1)
                    nc.vector.scalar_tensor_tensor(x[:, t, :], bank[7][:, 256:512], tg[:, 1:2], xb[:],
                                                   ALU.mult, ALU.add).then_inc(a.x_done, 1)

                def next_wait(t):
                    dve.wait_ge(a.x_done, t + 1)
                    after(dve, m.xn_ready, t)

                def next_stats(t):
                    chain.mark(nc.vector.bn_stats(stats2[:], x[:, t, :]))

                def next_mean(t):
                    chain.link(nc.vector.bn_aggr(mv2[:], stats2[:]))
                    nc.vector.tensor_scalar(ve2[:], mv2[:, 1:2], EPS, None, ALU.add).then_inc(m.var_ready, 1)

                def next_apply(t):
                    dve.wait_ge(m.rstd_ready, t + 1)
                    after(dve, m.xt_done, t)
                    nc.vector.tensor_scalar(xm[:], x[:, t, :], mv2[:, 0:1], rstd2[:], ALU.subtract, ALU.mult
                                            ).then_inc(m.xn_ready, 1)

                def nothing():
                    pass

                def body0(t):
                    def sequence_before(b2, stats_of=None):
                        if live(t - 1):
                            normalise(t - 1, b2, stats_of)
                        elif stats_of is not None:
                            next_wait(stats_of)
                            next_stats(stats_of)
                            chain.wait()

                    def apply_before():
                        if live(t - 2):
                            next_apply(t - 2)

                    def norm_ahead():
                        if live(t + 2):
                            layer_norm(t + 2)

                    n = a.units * t
                    steps = [lambda: sequence_before(0, t - 2 if live(t - 2) else None), apply_before,
                             lambda: sequence_before(1), norm_ahead]
                    for u in range(4):
                        if live(t):
                            shift(n + u, u % 2, steps[u])
                        else:
                            steps[u]()
                        if u == 0 and live(t - 2):
                            next_mean(t - 2)

                def body1(t):
                    n = a.units * t
                    if live(t):
                        shift(n, 0, (lambda: layer_norm(t + 2)) if live(t + 2) else nothing)
                    if live(t - 3):
                        next_apply(t - 3)
                    if live(t - 1):
                        normalise(t - 1, 0)
                    if live(t):
                        shift(n + 1, 1, nothing)
                    if live(t - 2):
                        residual(t - 2)
                    stats_of = t - 2 if live(t - 2) else None
                    if live(t - 1):
                        normalise(t - 1, 1, stats_of)
                    elif stats_of is not None:
                        next_wait(stats_of)
                        next_stats(stats_of)
                        chain.wait()
                    if stats_of is not None:
                        next_mean(stats_of)

                body = body0 if a.layer == 0 else body1

                for part, (t0, t1) in enumerate(((0, AHEAD), (AHEAD, TT))):
                    if before is None:
                        dve.wait_ge(x_loaded[part], 16)
                    ln_stats(a, chain, before, t0, t1)
                    nc.vector.tensor_scalar(ve[:, t0:t1].unsqueeze(2), mv[:, t0:t1, 1:2], EPS, None, ALU.add
                                            ).then_inc(a.var_ready, 1)
                    if part == 0:
                        if before is None:
                            dve.wait_ge(k_loaded, 64)
                        for t in range(AHEAD):
                            if before is None:
                                dve.wait_ge(kh_ready if t == 0 else kl_ready, 1)
                                keys(nc.vector, a, 0, t, k0_ready)
                            if t == 0:
                                dve.wait_ge(a.rstd_ready, 1)
                            layer_norm(t)
                for t in range(a.lag):
                    body(t)
                at0 = chain.n
                links = a.units + 4
                with dve.Fori(a.lag, TT - AHEAD) as t:
                    chain.at(at0 + (t - a.lag) * links)
                    body(t)
                    assert chain.n == links
                chain.at(at0 + (TT - AHEAD - a.lag) * links)
                for t in range(TT - AHEAD, TT + a.lag):
                    body(t)

            def feed_forward(m, before):
                chain = Chain(dve, R.chain)
                if m.layer == 0:
                    dve.wait_ge(w_const, 16 * 6)
                    nc.vector.tensor_scalar(sdt[:], sd[:], tg[:, 2:3], None, ALU.mult).then_inc(sdt_ready, 1)
                    nc.vector.tensor_scalar(bcb[:], bcb[:], tg[:, 1:2], None, ALU.mult).then_inc(bcb_ready, 1)
                    nc.vector.tensor_copy(gwh[:], gw[:]).then_inc(R.gw_split, 1)
                    dve.wait_ge(R.gw_split, 1)
                    nc.vector.tensor_tensor(gwl[:], gw[:], gwh[:].bitcast(F32), ALU.subtract).then_inc(R.gw_split, 1)
                else:
                    dve.wait_ge(R.sel_loaded, 16)
                    nc.vector.tensor_copy(sel, sel_raw).then_inc(R.sel_ready, 1)
                    dve.wait_ge(R.logits_done, 1)
                    chain.link(nc.vector.tensor_copy(lg, bank[4][:, 2 * P:4 * P].rearrange(
                        "p (t e) -> p t e", e=EXPERTS)))
                    for t in range(TT):
                        last = nc.vector.max(top[:, t, :], lg[:, t, :])
                    chain.link(last)
                    nc.vector.tensor_tensor(ew, lg, top[:, :, 0:1].to_broadcast([P, TT, EXPERTS]),
                                            ALU.subtract).then_inc(R.d_ready, 1)
                    for t in range(TT):
                        last = nc.vector.match_replace(rep[:, t, :], top[:, t, :], lg[:, t, :], NEG)
                    chain.link(last)
                    chain.link(nc.vector.tensor_tensor(rep, rep, lg, ALU.not_equal))
                    dve.wait_ge(R.e_ready, 1)
                    chain.link(nc.vector.tensor_tensor(ew, ew, rep, ALU.mult))
                    chain.link(nc.vector.reduce_sum(esum[:], ew, AX.X))
                    chain.link(nc.vector.reciprocal(esum[:], esum[:]))
                    nc.vector.tensor_tensor(ew, ew, esum[:].unsqueeze(2).to_broadcast([P, TT, EXPERTS]),
                                            ALU.mult).then_inc(R.w_ready, 1)
                    for k in range(NBLK):
                        dve.wait_ge(R.wt_hi, k + 1)
                        cols = slice(k * BLK, (k + 1) * BLK)
                        nc.vector.tensor_tensor(wts[EXPERTS:2 * EXPERTS, cols], bank[5 + k][0:EXPERTS, :],
                                                wts[0:EXPERTS, cols].bitcast(F32), ALU.subtract
                                                ).then_inc(R.wt_lo, 1)
                    for q in range(EXPERTS // EPQ):
                        dve.wait_ge(R.spread_done, NBLK * q + 2)
                        nc.vector.tensor_copy(mbc[:, q, BLK:2 * BLK], bank[MASK_BANKS[(2 * q + 1) % 4]][:]
                                              ).then_inc(R.mask_ready[1], 1)

                def body(i, first):
                    for cc in range(m.per_body):
                        c = i * m.per_body + cc
                        for k in range(NBLK):
                            n = NBLK * c + k
                            dve.wait_ge(m.s_ready, n + 1)
                            dve.wait_ge(m.u_done, n + 1)
                            if m.layer == 0:
                                nc.vector.scalar_tensor_tensor(h_t[:, k, :], bank[2 + k][:], su[:, c:c + 1],
                                                               s_t[:, k, :], ALU.mult, ALU.mult
                                                               ).then_inc(m.t_done, 1)
                                dve.wait_ge(m.t_done, n + 1)
                            else:
                                nc.vector.tensor_tensor(t_t[:], bank[2 + k][:], s_t[:, k, :], ALU.mult
                                                        ).then_inc(m.t_done, 1)
                                dve.wait_ge(m.t_done, n + 1)
                                if first and cc == 0:
                                    dve.wait_ge(R.mask_ready[k], EXPERTS // EPQ)
                                q = i * (m.per_body // CPQ) + cc // CPQ
                                nc.vector.tensor_tensor(h_t[:, k, :], t_t[:], mbc[:, q, k * BLK:(k + 1) * BLK],
                                                        ALU.mult).then_inc(m.h_full, 1)
                            dve.wait_ge(m.hh_ready, n + 1)
                            nc.vector.tensor_tensor(hl[:, k, :], h_t[:, k, :], hh[:, k, :].bitcast(F32),
                                                    ALU.subtract).then_inc(m.h_split, 1)
                body(0, True)
                if m.chunks > m.per_body:
                    with dve.Fori(1, m.chunks // m.per_body) as i:
                        body(i, False)
                dve.wait_ge(m.dn_done, NBLK * m.chunks)
                for h in range(KC):
                    scale = sdt[:, h:h + 1] if m.layer == 0 else tg[:, 3:4]
                    nc.vector.tensor_scalar(ot[:, h, BLK:2 * BLK], bank[5 + 2 * h][:], scale, None, ALU.mult
                                            ).then_inc(m.ot_ready[1], 1)
                for t in range(TT):
                    dve.wait_ge(m.back_done, t + 1)
                    nc.vector.tensor_tensor(x[:, t, :], bank[t % 2][:, 0:DM], x[:, t, :], ALU.add
                                            ).then_inc(m.x_done, 1)

            attention(A[0], M[0], None)
            feed_forward(M[0], A[0])
            attention(A[1], M[1], M[0])
            feed_forward(M[1], A[1])

        @block.tensor
        def _(pe):
            def product(o, w_sl, s, rh, rl, first, last, reopened=False):
                nc.tensor.matmul(o, wh[:, s, w_sl], rh, start=first, stop=False, skip_group_check=reopened)
                nc.tensor.matmul(o, wh[:, s, w_sl], rl, start=False, stop=False, skip_group_check=reopened)
                return nc.tensor.matmul(o, wl[:, s, w_sl], rh, start=False, stop=last, skip_group_check=reopened)

            def gate_up(m, n, c, s, k, fresh):
                if k == 0:
                    pe.wait_ge(m.w_split, c + 1)
                tok = slice(k * BLK, (k + 1) * BLK)
                for col, bk, free, done in ((0, k, m.s_ready, m.g_done), (DM, 2 + k, m.t_done, m.u_done)):
                    if not fresh:
                        pe.wait_ge(free, n - 1)
                    for h in range(KC):
                        last = product(bank[bk][:], slice(col + h * P, col + (h + 1) * P), s, xh[:, h, tok],
                                       xl[:, h, tok], h == 0, h == KC - 1)
                    last.then_inc(done, 1)

            def route_logits(m, t0, t1):
                for t in range(t0, t1):
                    pe.wait_ge(m.xt_split, t + 1)
                    tok = slice(t * P, (t + 1) * P)
                    for k in range(KC):
                        for i, (xs, ws) in enumerate(((xh, gwh), (xh, gwl), (xl, gwh))):
                            last = nc.tensor.matmul(bank[4][:, 2 * P + t * EXPERTS:2 * P + (t + 1) * EXPERTS], xs[:, k, tok],
                                                    ws[:, k, :], start=(k == 0 and i == 0),
                                                    stop=(k == KC - 1 and i == 2))
                if t1 == TT:
                    last.then_inc(R.logits_done, 1)

            def attention(a, m):
                def q_transposes(t):
                    pe.wait_ge(a.q_split, t + 1)
                    after(pe, a.q_ready, t)
                    if a.layer == 1:
                        after(pe, m.xtf_ready, t - 4)
                    for g in range(G):
                        last = nc.tensor.transpose(bank[6][:, g * P:(g + 1) * P],
                                                   qs[:, g, :, :].rearrange("p r d -> p (r d)").bitcast(F32), ident[:])
                    last.then_inc(a.q_transposed, 1)

                def scores(n, t, u):
                    if u == 0:
                        if a.layer == 0:
                            after(pe, a.k_ready, 2 * t)
                        else:
                            pe.wait_ge(a.k_ready, 2 * (t + 1))
                        pe.wait_ge(a.q_ready, t + 1)
                    after(pe, a.sub_done, n - 1)
                    b2, gps = a.unit(u)
                    for i, gp in enumerate(gps):
                        for r in range(2):
                            last = nc.tensor.matmul(bank[u % 2][:, i * a.ns:(i + 1) * a.ns],
                                                    qt[:, b2, 2 * gp:2 * gp + 2, :].rearrange("p g s -> p (g s)"),
                                                    a.kbd[:, r, 2 * t + b2, :], start=(r == 0), stop=(r == 1))
                    last.then_inc(a.scored, 1)

                def p_transposes(n, k):
                    pe.wait_ge(a.p_ready, n + 1)
                    after(pe, a.pts_ready, n - 1)
                    for j in range(4):
                        last = nc.tensor.transpose(bank[2 + k][:, j * P:(j + 1) * P], pt[:, k, j * P:(j + 1) * P],
                                                   ident[:])
                    last.then_inc(a.pt_done, 1)

                def values(n, t, u):
                    k = u % 2
                    b2, gps = a.unit(u)
                    pe.wait_ge(a.pts_ready, n + 1)
                    after(pe, a.y_done, 2 * t + b2 - 1)
                    if a.layer == 1 and b2 == 0 and isinstance(t, int) and t >= TT - 2:
                        route_logits(m, 0 if t == TT - 2 else t - 4, t - 3)
                    for j in range(4):
                        gp, pair = gps[j // a.npair], j % a.npair
                        last = nc.tensor.matmul(bank[4 + b2][:, gp * P:(gp + 1) * P], pts[:, k, j, :],
                                                a.vbd[:, 2 * t + b2, pair, :], start=(pair == 0),
                                                stop=(pair == a.npair - 1))
                    last.then_inc(a.av_done, 1)

                def y_transposes(t):
                    pe.wait_ge(a.y_done, 2 * (t + 1))
                    after(pe, a.x_done, t)
                    for k in range(KC):
                        last = nc.tensor.transpose(bank[7][:, k * P:(k + 1) * P], yt[:, k * P:(k + 1) * P], ident[:])
                    last.then_inc(a.yt_done, 1)

                def project(t):
                    pe.wait_ge(a.yts_ready, t + 1)
                    o = bank[7][:, 256:512]
                    for k in range(KC):
                        last = nc.tensor.matmul(o, yts[:, k, :], wc[:, k, :], start=(k == 0), stop=(k == KC - 1))
                    last.then_inc(a.proj_done, 1)

                def x_transposes(t):
                    pe.wait_ge(m.xn_ready, t + 1)
                    if a.layer == 1:
                        pe.wait_ge(a.q_ready, up_to(t + 5, TT))
                    after(pe, m.xtf_ready, t)
                    for k in range(KC):
                        last = nc.tensor.transpose(bank[a.x_bank][:, k * P:(k + 1) * P], xm[:, k * P:(k + 1) * P],
                                                   ident[:])
                    last.then_inc(m.xt_done, 1)

                def body(t):
                    if isinstance(t, int) and t == TT + 1:
                        pe.wait_ge(m.xt_split, TT // 2)
                        gate_up(m, 0, 0, 0, 0, True)
                    for u in range(a.units):
                        n = a.units * t + u
                        ahead = t if u + 2 < a.units else t + 1
                        if a.layer == 0 and u == 1 and live(t + 1):
                            q_transposes(t + 1)
                        if a.layer == 1 and u == 0 and live(t - 2):
                            project(t - 2)
                        if live(ahead) and live(t):
                            scores(n + 2, ahead, (u + 2) % a.units)
                        if live(t if u else t - 1):
                            values(n - 1, t if u else t - 1, (u - 1) % a.units)
                        if live(t):
                            p_transposes(n, u % 2)
                        if a.layer == 1 and u == 1 and live(t + 2):
                            q_transposes(t + 2)
                        if a.layer == 1 and u == 1 and live(t - 1):
                            y_transposes(t - 1)
                        if a.layer == 0 and u == 3 and live(t - 2):
                            x_transposes(t - 2)
                        if a.layer == 1 and u == 0 and live(t - 3):
                            x_transposes(t - 3)
                    if a.layer == 1 and isinstance(t, int) and t >= TT:
                        pe.wait_ge(a.y_done, 2 * TT)
                        route_logits(m, t - 4, t - 3)

                if a.layer == 0:
                    pe.wait_ge(k0_ready, 2)
                q_transposes(0)
                scores(0, 0, 0)
                scores(1, 0, 1)
                if a.layer == 1:
                    q_transposes(1)
                pe.wait_ge(a.v_ready, 2 * a.hk + 1)
                over_tiles(pe, a.lag, body)

            def feed_forward(m):
                def route_weights():
                    pe.wait_ge(R.w_ready, 1)
                    for t in range(TT):
                        last = nc.tensor.transpose(bank[5 + t // 4][0:EXPERTS, (t % 4) * P:(t % 4 + 1) * P],
                                                   ew[:, t, :], ident[:])
                    last.then_inc(R.wt_done, 1)

                def spread_weights():
                    pe.wait_ge(R.sel_ready, 1)
                    pe.wait_ge(R.wt_lo, NBLK)
                    for q in range(EXPERTS // EPQ):
                        for k in range(NBLK):
                            if q >= 2:
                                pe.wait_ge(R.mask_ready[k], q - 1)
                            nc.tensor.matmul(bank[MASK_BANKS[(2 * q + k) % 4]][:], sel[:, q * P:(q + 1) * P],
                                             wts[:, k * BLK:(k + 1) * BLK], start=True, stop=True
                                             ).then_inc(R.spread_done, 1)
                    for k in range(NBLK):
                        pe.wait_ge(R.mask_ready[k], EXPERTS // EPQ)

                def down(n, s, k, first):
                    pe.wait_ge(m.h_split, n + 1)
                    for h in range(KC):
                        ins = product(bank[4 + 2 * h + k][:], slice(2 * DM + h * P, 2 * DM + (h + 1) * P), s,
                                      hh[:, k, :], hl[:, k, :], first, True, reopened=True)
                    ins.then_inc(m.dn_done, 1)

                def body(i, first):
                    for cc in range(m.per_body):
                        c = i * m.per_body + cc
                        for k in range(NBLK):
                            n = NBLK * c + k
                            if first and n == 0:
                                continue
                            if first and n == 1:
                                pe.wait_ge(m.xt_split, TT)
                            gate_up(m, n, c, cc % WRING, k, first and cc == 0)
                            if m.layer == 1 and first and n == 1:
                                route_weights()
                                spread_weights()
                            if first and n == 1:
                                down(0, 0, 0, True)
                                continue
                            if not (first and n == 0):
                                down(n - 1, (cc if k else cc - 1) % WRING, 1 - k, first and n <= 2)
                body(0, True)
                if m.chunks > m.per_body:
                    with pe.Fori(1, m.chunks // m.per_body) as i:
                        body(i, False)
                down(NBLK * m.chunks - 1, (m.chunks - 1) % WRING, 1, False)
                for t in range(TT):
                    pe.wait_ge(m.ot_ready[t // 4], KC)
                    if t >= 2:
                        pe.wait_ge(m.x_done, t - 1)
                    for h in range(KC):
                        last = nc.tensor.transpose(bank[t % 2][:, h * P:(h + 1) * P], ot[:, h, t * P:(t + 1) * P],
                                                   ident[:])
                    last.then_inc(m.back_done, 1)

            pe.wait_ge(c_loaded, 16 * 3)
            attention(A[0], M[0])
            pe.wait_ge(w_const, 16 * 6)
            feed_forward(M[0])
            attention(A[1], M[1])
            feed_forward(M[1])



def kernel(x, ctx_512, g_xattn, g_ffn, L0_ffn_wq_gate, L0_ffn_s_gate, L0_ffn_wq_up, L0_ffn_s_up, L0_ffn_wq_down,
           L0_ffn_s_down, L1_xattn_Wc, L1_xattn_bc, L1_ffn_gate_w, L1_ffn_w_gate_proj, L1_ffn_w_up_proj,
           L1_ffn_w_down_proj):
    import numpy as np
    import concourse.bacc as bacc
    from concourse import mybir as mb
    from concourse.bass_utils import run_bass_kernel_spmd as run

    A = np.asarray

    def halves(rows, n):
        return rows.reshape(n, P, KC, P).transpose(0, 3, 2, 1).reshape(n, P, DM)

    def own_rows(heads):
        return np.tile(np.repeat(np.eye(heads, dtype=np.float32), 64 // heads, axis=0), (2, 1))

    pad = FFN_CHUNKS * P - HIDDEN
    gate0 = np.pad(A(L0_ffn_wq_gate), ((0, pad), (0, 0)))
    up0 = np.pad(A(L0_ffn_wq_up), ((0, pad), (0, 0)))
    down0 = np.pad(A(L0_ffn_wq_down).T, ((0, pad), (0, 0)))
    w0 = np.concatenate([halves(gate0, FFN_CHUNKS), halves(up0, FFN_CHUNKS), down0.reshape(FFN_CHUNKS, P, DM)], 2)
    s_gate = np.pad(A(L0_ffn_s_gate), (0, pad)).reshape(FFN_CHUNKS, P).T
    s_up = np.pad(A(L0_ffn_s_up), (0, pad)).reshape(FFN_CHUNKS, P).T

    def rows(w):
        return w.reshape(EXPERTS // EPQ, EPQ, CPQ, 32, DM).transpose(0, 2, 1, 3, 4).reshape(MOE_CHUNKS * P, DM)
    w1 = np.concatenate([halves(rows(A(L1_ffn_w_gate_proj)), MOE_CHUNKS), halves(rows(A(L1_ffn_w_up_proj)), MOE_CHUNKS),
                         rows(A(L1_ffn_w_down_proj).transpose(0, 2, 1)).reshape(MOE_CHUNKS, P, DM)], 2)
    ctx = A(ctx_512)
    ins = {
        "x_in": A(x).reshape(TOK, DM),
        "ctx_t": ctx.transpose(2, 0, 1).reshape(64, BATCH * KEYS),
        "ctx_in": ctx,
        "g_xattn": A(g_xattn),
        "g_ffn": A(g_ffn),
        "w0": w0,
        "s_gate": s_gate,
        "s_up": s_up,
        "s_down": A(L0_ffn_s_down).reshape(KC, P).T,
        "wc_t": A(L1_xattn_Wc).T,
        "bc": A(L1_xattn_bc),
        "gate_t": A(L1_ffn_gate_w).T,
        "w1": w1,
        "ident_in": np.eye(P, dtype=np.float32),
        "kmask0": own_rows(8),
        "kmask1": own_rows(4),
        "sel_in": np.tile(np.repeat(np.eye(EXPERTS, dtype=np.float32), 32, axis=1), (2, 1)),
    }
    nc = bacc.Bacc("TRN2", target_bir_lowering=False, num_devices=1)
    arrays, args = {}, []
    for name, a in ins.items():
        a = np.ascontiguousarray(a)
        arrays[name] = a
        args.append(nc.dram_tensor(name, a.shape, mb.dt.from_np(a.dtype), kind="ExternalInput").ap())
    args.append(nc.dram_tensor("out", (TOK, DM), F32, kind="ExternalOutput").ap())
    build(nc, *args)
    r = run(nc, [arrays], core_ids=[0])
    return r.results[0]["out"].reshape(BATCH, SEQ, DM)
```

```python
from contextlib import ExitStack

import concourse.bass as bass
from concourse import mybir

ALU = mybir.AluOpType
ACT = mybir.ActivationFunctionType
AX = mybir.AxisListType
F32 = mybir.dt.float32
F32R = mybir.dt.float32r
I32 = mybir.dt.int32

P = 128
DM = 256
KC = DM // P
COLS = 512
TT = 8
TOK = TT * P
BATCH = 16
SEQ = 64
KEYS = 64
G = 4
BLK = 512
NBLK = TOK // BLK
EXPERTS = 32
INNER = 96
TOPK = 8
EPQ = 4
CPQ = EPQ * INNER // P
MOE_CHUNKS = EXPERTS * INNER // P
WPACK = 3 * DM
WRING = 3
EPS = 1e-5
ZERO_POINT = 128.0
HIDDEN = 704
FFN_CHUNKS = (HIDDEN + P - 1) // P
NEG = -3.0e38
W_EARLY = (TT - 2, TT - 1)
MASK_BANKS = (4, 7, 5, 6)
MASKS = NBLK * EXPERTS // EPQ
KEYS_AFTER = {3: (0, 2), 4: (2, 4), 5: (4, TT)}
AHEAD = 2


def after(eng, sem, value):
    if not (isinstance(value, int) and value <= 0):
        eng.wait_ge(sem, value)


def live(t):
    return not isinstance(t, int) or 0 <= t < TT


def on_vector(j):
    return j % 4 == 1


def masks_out(j):
    return sum(on_vector(i) == on_vector(j) for i in range(j + 1))


def early(t):
    return isinstance(t, int) and t in W_EARLY


def up_to(value, most):
    return min(value, most) if isinstance(value, int) else value


def over_tiles(eng, lag, body):
    for t in range(lag):
        body(t)
    with eng.Fori(lag, TT - AHEAD) as t:
        body(t)
    for t in range(TT - AHEAD, TT + lag):
        body(t)


class Chain:

    def __init__(self, eng, sem):
        self.eng, self.sem, self.base, self.n = eng, sem, 0, 0

    def at(self, base):
        self.base, self.n = base, 0

    def mark(self, ins):
        ins.then_inc(self.sem, 1)
        self.n += 1

    def now(self):
        return self.base + self.n

    def wait(self, value=None):
        self.eng.wait_ge(self.sem, self.now() if value is None else value)

    def link(self, ins):
        self.mark(ins)
        self.wait()


class Attention:

    def __init__(self, layer, kv_heads, kbd, vbd, sb, sem):
        self.layer, self.hk = layer, kv_heads
        self.d = DM // G // kv_heads
        self.ns = kv_heads * KEYS
        self.npair = kv_heads // 2
        self.gpu = COLS // self.ns
        self.units = 2 * (G // 2) // self.gpu
        self.lag = 3 if layer == 0 else 4
        self.x_bank = 7 if layer == 0 else 6
        self.scale = float(self.d) ** -0.5
        n = f"a{layer}_"
        self.kbd = kbd[:, :, :].rearrange("p r (b n) -> p r b n", n=self.ns)
        self.vbd = vbd[:, 0:BATCH * self.npair * P].rearrange("p (b j c) -> p b j c", j=self.npair, c=P)
        self.kmask = sb(n + "kmask", [P, self.hk])
        self.k_ready = sem(n + "k_ready")
        self.v_ready = sem(n + "v_ready")
        self.var_ready = sem(n + "var_ready")
        self.rstd_ready = sem(n + "rstd_ready")
        self.xn_ready = sem(n + "xn_ready")
        self.qh_ready = sem(n + "qh_ready")
        self.q_split = sem(n + "q_split")
        self.q_transposed = sem(n + "q_transposed")
        self.q_ready = sem(n + "q_ready")
        self.scored = sem(n + "scored")
        self.sub_done = sem(n + "sub_done")
        self.p_ready = sem(n + "p_ready")
        self.pt_done = sem(n + "pt_done")
        self.pts_ready = sem(n + "pts_ready")
        self.av_done = sem(n + "av_done")
        self.y_done = sem(n + "y_done")
        self.x_done = sem(n + "x_done")
        self.xb_ready = sem(n + "xb_ready")
        self.yt_done = sem(n + "yt_done")
        self.yts_ready = sem(n + "yts_ready")
        self.proj_done = sem(n + "proj_done")
        self.dve_chain = sem(n + "dve_chain")

    def unit(self, u):
        return (u // 2, [u % 2]) if self.gpu == 1 else (u, [0, 1])


class Mlp:

    def __init__(self, layer, chunks, per_body, sem):
        self.layer, self.chunks, self.per_body = layer, chunks, per_body
        n = f"m{layer}_"
        self.var_ready = sem(n + "var_ready")
        self.rstd_ready = sem(n + "rstd_ready")
        self.xn_ready = sem(n + "xn_ready")
        self.xt_done = sem(n + "xt_done")
        self.xtf_ready = sem(n + "xtf_ready")
        self.xh_ready = sem(n + "xh_ready")
        self.xt_split = sem(n + "xt_split")
        self.wf_ready = sem(n + "wf_ready")
        self.wh_ready = sem(n + "wh_ready")
        self.w_split = sem(n + "w_split")
        self.g_done = sem(n + "g_done")
        self.u_done = sem(n + "u_done")
        self.s_ready = sem(n + "s_ready")
        self.t_done = sem(n + "t_done")
        self.h_full = self.t_done if layer == 0 else sem(n + "h_full")
        self.hh_ready = sem(n + "hh_ready")
        self.h_split = sem(n + "h_split")
        self.dn_done = sem(n + "dn_done")
        self.ot_ready = [sem(n + f"ot_ready{k}") for k in range(NBLK)]
        self.back_done = sem(n + "back_done")
        self.x_done = sem(n + "x_done")
        self.dve_chain = sem(n + "dve_chain")
        self.w_loaded = [sem(n + f"w_loaded{i}") for i in range(2)]


class Route:

    def __init__(self, sem):
        self.gw_split = sem("r_gw_split")
        self.logits_done = sem("r_logits_done")
        self.d_ready = sem("r_d_ready")
        self.e_ready = sem("r_e_ready")
        self.w_ready = sem("r_w_ready")
        self.wt_done = sem("r_wt_done")
        self.wt_hi = sem("r_wt_hi")
        self.wt_lo = sem("r_wt_lo")
        self.sel_loaded = sem("r_sel_loaded")
        self.sel_ready = sem("r_sel_ready")
        self.spread_done = sem("r_spread_done")
        self.mask_ready = [sem("r_mask_ready0"), sem("r_mask_ready1")]
        self.chain = sem("r_chain")


def build(nc, x_in, ctx_t, ctx_in, g_xattn, g_ffn, w0, s_gate, s_up, s_down, wc_t, bc, gate_t, w1, ident_in,
          kmask0, kmask1, sel_in, out):
    with ExitStack() as stack:
        def sb(name, shape, dt=F32):
            return stack.enter_context(nc.sbuf_tensor(name, shape, dt))

        def sem(name):
            return stack.enter_context(nc.semaphore(name))

        kbd0 = sb("kbd0", [P, 2, BATCH * 8 * KEYS], F32R)
        kbd1 = kbd0[:, 1].rearrange("p (r n) -> p r n", r=2)
        vbd = sb("vbd", [P, BATCH * 4 * P])
        A = [Attention(0, 8, kbd0, vbd, sb, sem), Attention(1, 4, kbd1, vbd, sb, sem)]
        R = Route(sem)
        M = [Mlp(0, FFN_CHUNKS, FFN_CHUNKS, sem), Mlp(1, MOE_CHUNKS, 2 * CPQ, sem)]

        x = sb("x", [P, TT, DM])
        ident = sb("ident", [P, P])
        ctx_k = sb("ctx_k", [P, BATCH, KEYS])
        kh = sb("kh", [P, BATCH, KEYS], F32R)
        kl = sb("kl", [P, BATCH, KEYS])
        ctx_v = sb("ctx_v", [P, BATCH, 64])
        tg = sb("tg", [P, 4])
        sg = sb("sg", [P, FFN_CHUNKS])
        su = sb("su", [P, FFN_CHUNKS])
        sd = sb("sd", [P, KC])
        sdt = sb("sdt", [P, KC])
        wc = sb("wc", [P, KC, DM])
        bcb = sb("bcb", [P, DM])
        gw = sb("gw", [P, KC, EXPERTS])
        gwh = sb("gwh", [P, KC, EXPERTS], F32R)
        gwl = sb("gwl", [P, KC, EXPERTS], F32R)
        stats = sb("stats", [P, TT, 6])
        mv = sb("mv", [P, TT, 2])
        ve = sb("ve", [P, TT])
        neghalf = sb("neghalf", [P, TT])
        idle = sb("idle", [P, 2])
        one = sb("one", [P, 1])
        rstd = sb("rstd", [P, TT])
        xn = sb("xn", [P, DM])
        stats2 = sb("stats2", [P, 6])
        mv2 = sb("mv2", [P, 2])
        ve2 = sb("ve2", [P, 1])
        rstd2 = sb("rstd2", [P, 1])
        xm = sb("xm", [P, DM])
        xb = sb("xb", [P, DM])
        qs = sb("qs", [P, G, 2, 64], F32R)
        qt = sb("qt", [P, 2, G, SEQ], F32R)
        mx = sb("mx", [P, 2, 8])
        dt_pt = sb("dt_pt", [P, 2, 2, 512])
        dt_, pt = dt_pt[:, 0], dt_pt[:, 1]
        pts = sb("pts", [P, 2, 4, P])
        rc = sb("rc", [P, 2, 16])
        yt = sb("yt", [P, DM])
        yts = sb("yts", [P, KC, P])
        xtf = sb("xtf", [P, KC, P])
        xh = sb("xh", [P, KC, TOK], F32R)
        xl = sb("xl", [P, KC, TOK], F32R)
        wraw = sb("wraw", [P, 2, WPACK])
        wrawi = wraw[:].bitcast(I32)
        wf = sb("wf", [P, 2, WPACK])
        wh = sb("wh", [P, WRING, WPACK], F32R)
        wl = sb("wl", [P, WRING, WPACK], F32R)
        s_t = pts[:].rearrange("p k j c -> p k (j c)")
        t_t = sb("t_t", [P, BLK])
        h_t = sb("h_t", [P, 2, BLK])
        hh = sb("hh", [P, 2, BLK], F32R)
        hl = sb("hl", [P, 2, BLK], F32R)
        ot = dt_pt[:].rearrange("p a b n -> p a (b n)")
        top = sb("top", [P, TT, TOPK])
        esum = sb("esum", [P, TT])
        te = TT * EXPERTS
        free = vbd[:, BATCH * A[1].npair * P:]
        lg, rep, ew = (free[:, i * te:(i + 1) * te].rearrange("p (t e) -> p t e", e=EXPERTS) for i in range(3))
        sel_raw = free[0:2 * EXPERTS, TOK:2 * TOK]
        sel = kbd0[0:2 * EXPERTS, 0, 0:TOK]
        wts = kbd0[0:2 * EXPERTS, 0, TOK:2 * TOK]
        mbc = vbd[:].rearrange("p (q t) -> p q t", q=EXPERTS // EPQ)

        def mask(j):
            return mbc[:, j // NBLK, (j % NBLK) * BLK:(j % NBLK + 1) * BLK]

        bank = [stack.enter_context(nc.psum_tensor(f"bank{i}", [P, 512], F32)) for i in range(8)]

        x_loaded = [sem("x_loaded0"), sem("x_loaded1")]
        k_loaded = sem("k_loaded")
        v_loaded = sem("v_loaded")
        c_loaded = sem("c_loaded")
        w_const = sem("w_const")
        neg_ready = sem("neg_ready")
        tanh_ready = sem("tanh_ready")
        kh_ready = sem("kh_ready")
        v_zeroed = sem("v_zeroed")
        kl_ready = sem("kl_ready")
        k0_ready = sem("k0_ready")
        bcb_ready = sem("bcb_ready")
        sdt_ready = sem("sdt_ready")
        stored = sem("stored")

        block = stack.enter_context(nc.Block())

        def keys(ops, a, t, r, ready):
            b = bass.ds(2 * t, 2)
            shape = [P, 2, a.hk, KEYS]
            part = kh[:].bitcast(F32) if r == 0 else kl[:]
            ops.tensor_tensor(a.kbd[:, r, b, :].rearrange("p b (h t) -> p b h t", t=KEYS),
                              part[:, b, :].unsqueeze(2).to_broadcast(shape),
                              a.kmask[:].unsqueeze(1).unsqueeze(3).to_broadcast(shape), ALU.mult
                              ).then_inc(ready, 1)

        def value_ones(eng, ops, a):
            for i in range(a.hk):
                half = slice(64 * (i % 2), 64 * (i % 2) + 64)
                ops.memset(a.vbd[half, :, i // 2, 64 + i:65 + i], 1.0).then_inc(a.v_ready, 1)
                eng.wait_ge(a.v_ready, i + 1)

        @block.sync
        def _(sp):
            x_v = x_in.rearrange("(t p) d -> p t d", p=P)
            sp.dma_start(x[:, 0:2, :], x_v[:, 0:2, :]).then_inc(x_loaded[0], 16)
            for half in range(2):
                sp.dma_start(ctx_k[64 * half:64 * half + 64], ctx_t.rearrange("p (b t) -> p b t", t=KEYS)
                             ).then_inc(k_loaded, 16)
            sp.dma_start(A[0].kmask[:], kmask0).then_inc(k_loaded, 16)
            sp.dma_start(ident[:], ident_in).then_inc(c_loaded, 16)
            for dst, src in ((tg[:, 0:2], g_xattn), (tg[:, 2:4], g_ffn)):
                sp.dma_start(dst, src.rearrange("(a n) -> a n", a=1).to_broadcast([P, 2])).then_inc(c_loaded, 16)
            sp.dma_start(x[:, 2:TT, :], x_v[:, 2:TT, :]).then_inc(x_loaded[1], 16)
            for half in range(2):
                sp.dma_start(ctx_v[64 * half:64 * half + 64], ctx_in.rearrange("b t d -> t b d")
                             ).then_inc(v_loaded, 16)
            for dst, src in ((sg[:], s_gate), (su[:], s_up), (sd[:], s_down),
                             (wc[:], wc_t.rearrange("(k p) n -> p k n", p=P)),
                             (bcb[:], bc.rearrange("(a n) -> a n", a=1).to_broadcast([P, DM])),
                             (gw[:], gate_t.rearrange("(k p) n -> p k n", p=P)), (A[1].kmask[:], kmask1)):
                sp.dma_start(dst, src).then_inc(w_const, 16)

            def stream(m, raw, dram):
                def chunk(i, cc, first):
                    c = i * m.per_body + cc
                    if not (first and cc < 2):
                        sp.wait_ge(m.wf_ready if m.layer == 0 else m.w_split, c - 1)
                    sp.dma_start(raw[:, cc % 2, :], dram[bass.ds(c, 1)].rearrange("a p n -> (a p) n")
                                 ).then_inc(m.w_loaded[cc % 2], 16)
                for cc in range(m.per_body):
                    chunk(0, cc, True)
                if m.chunks > m.per_body:
                    with sp.Fori(1, m.chunks // m.per_body) as i:
                        for cc in range(m.per_body):
                            chunk(i, cc, False)

            stream(M[0], wrawi, w0)
            sp.wait_ge(M[0].w_split, FFN_CHUNKS)
            sp.wait_ge(A[0].av_done, A[0].units * TT)
            sp.dma_start(sel_raw, sel_in).then_inc(R.sel_loaded, 16)
            stream(M[1], wraw, w1)
            out_v = out.rearrange("(t p) d -> p t d", p=P)
            for t in range(TT):
                sp.wait_ge(M[1].x_done, t + 1)
                sp.dma_start(out_v[:, t, :], x[:, t, :]).then_inc(stored, 16)
            sp.wait_ge(stored, 16 * TT)

        @block.gpsimd
        def _(pool):
            nc.gpsimd.memset(neghalf[:], -0.5).then_inc(neg_ready, 1)
            nc.gpsimd.memset(one[:], 1.0).then_inc(neg_ready, 1)

            def power(m, t, dst, src):
                pool.wait_ge(m.var_ready, t + 1)
                nc.gpsimd.tensor_tensor(dst, src, neghalf[:, 0:src.shape[-1]], ALU.pow).then_inc(m.rstd_ready, 1)

            def q_split(a, t):
                src = xn[:].rearrange("p (g d) -> p g d", g=G)
                pool.wait_ge(a.xn_ready, t + 1)
                after(pool, a.q_transposed, t)
                nc.gpsimd.tensor_tensor(qs[:, :, 0, :], src, one[:].unsqueeze(2).to_broadcast([P, G, 64]),
                                        ALU.mult).then_inc(a.qh_ready, 1)
                pool.wait_ge(a.qh_ready, t + 1)
                nc.gpsimd.tensor_tensor(qs[:, :, 1, :], src, qs[:, :, 0, :].bitcast(F32), ALU.subtract
                                        ).then_inc(a.q_split, 1)

            def both_keys(a, t0, t1):
                for t in range(t0, t1):
                    for r in range(2):
                        keys(nc.gpsimd, a, t, r, a.k_ready)

            def w_lo(m, c, cc):
                src = wf if m.layer == 0 else wraw
                pool.wait_ge(m.wh_ready, c + 1)
                nc.gpsimd.tensor_tensor(wl[:, cc % WRING, :], src[:, cc % 2, :], wh[:, cc % WRING, :].bitcast(F32),
                                        ALU.subtract).then_inc(m.w_split, 1)

            def attention(a, m):
                def x_split(t):
                    tok = bass.ds(t * P, P)
                    pool.wait_ge(m.xtf_ready, t + 1)
                    nc.gpsimd.tensor_tensor(xh[:, :, tok], xtf[:], one[:].unsqueeze(2).to_broadcast([P, KC, P]),
                                            ALU.mult).then_inc(m.xh_ready, 1)
                    pool.wait_ge(m.xh_ready, t + 1)
                    nc.gpsimd.tensor_tensor(xl[:, :, tok], xtf[:], xh[:, :, tok].bitcast(F32), ALU.subtract
                                            ).then_inc(m.xt_split, 1)

                def add_output(t):
                    pool.wait_ge(a.y_done, 2 * (t + 1))
                    nc.gpsimd.tensor_tensor(x[:, t, :], x[:, t, :], yt[:], ALU.add).then_inc(a.x_done, 1)

                def add_bias(t):
                    after(pool, a.x_done, t)
                    nc.gpsimd.tensor_tensor(xb[:], x[:, t, :], bcb[:], ALU.add).then_inc(a.xb_ready, 1)

                def body(t):
                    tile_steps(t)
                    if early(t):
                        w_lo(m, W_EARLY.index(t), W_EARLY.index(t))

                def tile_steps(t):
                    if a.layer == 0:
                        if live(t - 3):
                            x_split(t - 3)
                        if live(t - 2):
                            power(m, t - 2, rstd2[:], ve2[:])
                        if live(t + 2):
                            keys(nc.gpsimd, a, t + 2, 0, a.k_ready)
                            q_split(a, t + 2)
                        if live(t - 1):
                            add_output(t - 1)
                        if live(t + 2):
                            keys(nc.gpsimd, a, t + 2, 1, a.k_ready)
                    else:
                        if live(t - 2):
                            add_bias(t - 2)
                        if live(t + 2):
                            q_split(a, t + 2)
                        if live(t - 2):
                            power(m, t - 2, rstd2[:], ve2[:])
                        if live(t - 3):
                            x_split(t - 3)

                if a.layer == 0:
                    pool.wait_ge(kl_ready, 2)
                    both_keys(a, 1, 2)
                else:
                    pool.wait_ge(bcb_ready, 1)
                    power(a, 0, rstd[:, 0:AHEAD], ve[:, 0:AHEAD])
                    q_split(a, 0)
                q_split(a, 1)
                power(a, 1, rstd[:, AHEAD:TT], ve[:, AHEAD:TT])
                over_tiles(pool, a.lag, body)

            def feed_forward(m):

                def body(i, first):
                    for cc in range(m.per_body):
                        if not (first and cc < len(W_EARLY)):
                            w_lo(m, i * m.per_body + cc, cc)
                            if m.layer == 0:
                                if cc == 2:
                                    pool.wait_ge(A[0].av_done, A[0].units * TT)
                                    nc.gpsimd.memset(A[1].vbd, 0.0).then_inc(v_zeroed, 1)
                                    pool.wait_ge(v_zeroed, 3)
                                    value_ones(pool, nc.gpsimd, A[1])
                                    pool.wait_ge(w_const, 16 * 7)
                                else:
                                    both_keys(A[1], *KEYS_AFTER[cc])
                body(0, True)
                if m.chunks > m.per_body:
                    with pool.Fori(1, m.chunks // m.per_body) as i:
                        body(i, False)

            pool.wait_ge(neg_ready, 2)
            nc.gpsimd.memset(A[0].vbd[:, 0:BATCH // 2], 0.0).then_inc(v_zeroed, 1)
            power(A[0], 0, rstd[:, 0:AHEAD], ve[:, 0:AHEAD])
            q_split(A[0], 0)
            pool.wait_ge(kh_ready, 1)
            for b in (slice(0, 2), slice(2, BATCH)):
                nc.gpsimd.tensor_tensor(kl[:, b], ctx_k[:, b], kh[:, b].bitcast(F32), ALU.subtract
                                        ).then_inc(kl_ready, 1)
            attention(A[0], M[0])
            feed_forward(M[0])
            attention(A[1], M[1])
            feed_forward(M[1])

        @block.scalar
        def _(act):
            act.wait_ge(neg_ready, 2)
            half = A[0].vbd[:, BATCH // 2:BATCH].rearrange("p b j c -> p (b j c)")
            nc.scalar.activation(half, one[:].to_broadcast([P, BATCH // 2 * A[0].npair * P]), ACT.Copy, scale=0.0
                                 ).then_inc(v_zeroed, 1)
            act.wait_ge(k_loaded, 48)
            nc.scalar.activation(kh[:], ctx_k[:], ACT.Copy).then_inc(kh_ready, 1)
            act.wait_ge(c_loaded, 48)
            nc.scalar.activation(tg[:], tg[:], ACT.Tanh).then_inc(tanh_ready, 1)

            def load_table(func, col):
                nc.scalar.activation(idle[:, col:col + 1], one[:], func)

            def w_hi(m, c, cc=None, i=0):
                cc = c if cc is None else cc
                act.wait_ge(m.w_loaded[cc % 2], 16 * (i * (m.per_body // 2) + cc // 2 + 1))
                src = wraw
                if m.layer == 0:
                    after(act, m.w_split, c - 1)
                    nc.scalar.activation(wf[:, cc % 2, :], wrawi[:, cc % 2, :], ACT.Copy, bias=-ZERO_POINT
                                         ).then_inc(m.wf_ready, 1)
                    act.wait_ge(m.wf_ready, c + 1)
                    src = wf
                after(act, m.dn_done, NBLK * (c - WRING + 1))
                nc.scalar.activation(wh[:, cc % WRING, :], src[:, cc % 2, :], ACT.Copy).then_inc(m.wh_ready, 1)

            def values(a):
                act.wait_ge(a.v_ready, a.hk)
                if a.layer == 0:
                    act.wait_ge(tanh_ready, 1)
                    act.wait_ge(v_loaded, 32)
                for i in range(a.hk):
                    half = slice(64 * (i % 2), 64 * (i % 2) + 64)
                    cols = slice(i * a.d, (i + 1) * a.d)
                    scale = tg[half, 0:1] if a.layer == 0 else 1.0
                    nc.scalar.activation(a.vbd[half, :, i // 2, cols], ctx_v[half, :, cols], ACT.Copy, scale=scale
                                         ).then_inc(a.v_ready, 1)

            def attention(a, m):
                def q_copy(t):
                    act.wait_ge(a.q_transposed, t + 1)
                    after(act, a.scored, a.units * t)
                    nc.scalar.activation(qt[:], bank[6][:].rearrange("p (g b s) -> p b g s", b=2, s=SEQ), ACT.Copy
                                         ).then_inc(a.q_ready, 1)

                def exp(n, k):
                    act.wait_ge(a.sub_done, n + 1)
                    after(act, a.pt_done, n - 1)
                    nc.scalar.activation(pt[:, k, :], dt_[:, k, :], ACT.Exp, scale=a.scale).then_inc(a.p_ready, 1)

                def pt_copy(n, k):
                    act.wait_ge(a.pt_done, n + 1)
                    after(act, a.av_done, n - 1)
                    for j in (0, 2):
                        nc.scalar.activation(pts[:, k, j:j + 2, :], bank[2 + k][:, j * P:(j + 2) * P].rearrange(
                            "p (j c) -> p j c", c=P), ACT.Copy).then_inc(a.pts_ready, 1)

                def yt_copy(t):
                    act.wait_ge(a.yt_done, t + 1)
                    after(act, a.proj_done, t)
                    nc.scalar.activation(yts[:], bank[7][:, 0:DM].rearrange("p (k c) -> p k c", c=P), ACT.Copy
                                         ).then_inc(a.yts_ready, 1)

                def xt_copy(t):
                    act.wait_ge(m.xt_done, t + 1)
                    after(act, m.xt_split, t)
                    nc.scalar.activation(xtf[:], bank[a.x_bank][:, 0:DM].rearrange("p (k c) -> p k c", c=P), ACT.Copy
                                         ).then_inc(m.xtf_ready, 1)

                def body(t):
                    for u in range(a.units):
                        n = a.units * t + u
                        if a.layer == 1 and u == 1 and live(t - 3):
                            xt_copy(t - 3)
                        if u == a.units - 2 and live(t + 1):
                            q_copy(t + 1)
                        if a.layer == 1 and u == 0 and live(t - 2):
                            yt_copy(t - 2)
                        if live(t if u else t - 1):
                            pt_copy(n - 1, (u + 1) % 2)
                        if live(t):
                            exp(n, u % 2)
                        if a.layer == 0 and u == 0 and live(t - 3):
                            xt_copy(t - 3)
                        if u == a.units // 2 and early(t):
                            w_hi(m, W_EARLY.index(t))

                if a.layer == 1:
                    values(a)
                q_copy(0)
                if a.layer == 0:
                    values(a)
                over_tiles(act, a.lag, body)
                if a.layer == 0:
                    load_table(ACT.Silu, 1)

            def feed_forward(m):
                if m.layer == 0:
                    act.wait_ge(w_const, 16 * 7)

                def gate(n, c, k):
                    act.wait_ge(m.g_done, n + 1)
                    after(act, m.t_done, n - 1)
                    scale = sg[:, c:c + 1] if m.layer == 0 else 1.0
                    nc.scalar.activation(s_t[:, k, :], bank[k][:], ACT.Silu, scale=scale).then_inc(m.s_ready, 1)

                def route():
                    act.wait_ge(R.d_ready, 1)
                    nc.scalar.activation(ew, ew, ACT.Exp).then_inc(R.e_ready, 1)
                    for k in range(NBLK):
                        gate(k, 0, k)
                    act.wait_ge(R.wt_done, 1)
                    for k in range(NBLK):
                        nc.scalar.activation(wts[0:EXPERTS, k * BLK:(k + 1) * BLK], bank[5 + k][0:EXPERTS, :], ACT.Copy
                                             ).then_inc(R.wt_hi, 1)
                    for j in range(MASKS):
                        if not on_vector(j):
                            act.wait_ge(R.spread_done, j + 1)
                            nc.scalar.activation(mask(j), bank[MASK_BANKS[j % 4]][:], ACT.Copy
                                                 ).then_inc(R.mask_ready[0], 1)
                        if j in (3, 7):
                            round_h(j // 4, j // 4, True)

                def round_h(n, k, fresh):
                    act.wait_ge(m.h_full, n + 1)
                    if not fresh:
                        act.wait_ge(m.dn_done, n - 1)
                    nc.scalar.activation(hh[:, k, :], h_t[:, k, :], ACT.Copy).then_inc(m.hh_ready, 1)

                def body(i, first, last):
                    for cc in range(m.per_body):
                        c = i * m.per_body + cc
                        for k in range(NBLK):
                            n = NBLK * c + k
                            fresh = first and cc == 0
                            if not (fresh and m.layer == 1):
                                gate(n, c, k)
                            ready = first and cc + 1 < len(W_EARLY)
                            if k == 0 and not ready and not (last and cc == m.per_body - 1):
                                w_hi(m, c + 1, (cc + 1) % m.per_body, i + (cc + 1) // m.per_body)
                            if not (fresh and m.layer == 1):
                                round_h(n, k, fresh)
                if m.layer == 1:
                    route()
                bodies = m.chunks // m.per_body
                body(0, True, bodies == 1)
                if bodies > 1:
                    with act.Fori(1, bodies - 1) as i:
                        body(i, False, False)
                    body(bodies - 1, False, True)
                if m.layer == 0:
                    act.wait_ge(sdt_ready, 1)
                act.wait_ge(m.dn_done, NBLK * m.chunks - 1)
                for h in range(KC):
                    scale = sdt[:, h:h + 1] if m.layer == 0 else tg[:, 3:4]
                    nc.scalar.activation(ot[:, h, 0:BLK], bank[4 + 2 * h][:], ACT.Copy, scale=scale
                                         ).then_inc(m.ot_ready[0], 1)
                act.wait_ge(m.dn_done, NBLK * m.chunks)
                scale = sdt[:, 0:1] if m.layer == 0 else tg[:, 3:4]
                nc.scalar.activation(ot[:, 0, BLK:2 * BLK], bank[5][:], ACT.Copy, scale=scale
                                     ).then_inc(m.ot_ready[1], 1)
                if m.layer == 0:
                    load_table(ACT.Exp, 0)

            attention(A[0], M[0])
            feed_forward(M[0])
            attention(A[1], M[1])
            feed_forward(M[1])

        @block.vector
        def _(dve):
            chains = [Chain(dve, a.dve_chain) for a in A]

            def ln_stats(a, before, t0, t1):
                chain = chains[a.layer]
                for t in range(t0, t1):
                    if before is not None:
                        dve.wait_ge(before.x_done, t + 1)
                    last = nc.vector.bn_stats(stats[:, t, :], x[:, t, :])
                chain.link(last)
                for t in range(t0, t1):
                    last = nc.vector.bn_aggr(mv[:, t, :], stats[:, t, :])
                chain.link(last)
                nc.vector.tensor_scalar(ve[:, t0:t1].unsqueeze(2), mv[:, t0:t1, 1:2], EPS, None, ALU.add
                                        ).then_inc(a.var_ready, 1)

            def layer_norm(a, t):
                if isinstance(t, int) and t == AHEAD:
                    dve.wait_ge(a.rstd_ready, 2)
                after(dve, a.q_split, t)
                nc.vector.tensor_scalar(xn[:].rearrange("p (g h d) -> p h g d", g=G, d=a.d),
                                        x[:, t, :].rearrange("p (h g d) -> p h g d", g=G, d=a.d),
                                        mv[:, t, 0:1], rstd[:, bass.ds(t, 1)], ALU.subtract, ALU.mult
                                        ).then_inc(a.xn_ready, 1)

            def attention(a, m, before):
                chain = chains[a.layer]

                def shift(n, k, between):
                    dve.wait_ge(a.scored, n + 1)
                    s = bank[k][:].rearrange("p (h t) -> p h t", t=KEYS)
                    chain.mark(nc.vector.reduce_max(mx[:, k, :], s, AX.X))
                    done = chain.now()
                    between()
                    chain.wait(done)
                    after(dve, a.p_ready, n - 1)
                    nc.vector.tensor_tensor(dt_[:, k, :].rearrange("p (h t) -> p h t", t=KEYS), s,
                                            mx[:, k, :].unsqueeze(2).to_broadcast([P, 8, KEYS]),
                                            ALU.subtract).then_inc(a.sub_done, 1)

                def normalise(t, b2, stats_of=None):
                    q = 2 * t + b2
                    if stats_of is not None:
                        next_wait(stats_of)
                    dve.wait_ge(a.av_done, a.units // 2 * (q + 1))
                    o = bank[4 + b2][:, 0:2 * P].rearrange("p (i c) -> p i c", c=P)
                    rs = rc[:, b2, 0:2 * a.hk].rearrange("p (i h) -> p i h", i=2)
                    chain.mark(nc.vector.reciprocal(rs, o[:, :, 64:64 + a.hk]))
                    if stats_of is not None:
                        next_stats(stats_of)
                    chain.wait()
                    if b2 == 0:
                        after(dve, a.x_done if a.layer == 0 else a.yt_done, t)
                    for g2 in range(2):
                        pi, po = slice(64 * g2, 64 * g2 + 64), slice(64 * b2, 64 * b2 + 64)
                        last = nc.vector.tensor_tensor(
                            yt[po].rearrange("p (h i g d) -> p i h g d", h=a.hk, i=2, g=2)[:, :, :, g2, :],
                            o[pi, :, 0:64].rearrange("p i (h d) -> p i h d", d=a.d),
                            rs[pi].unsqueeze(3).to_broadcast([64, 2, a.hk, a.d]), ALU.mult)
                    last.then_inc(a.y_done, 1)

                def residual(t):
                    dve.wait_ge(a.xb_ready, t + 1)
                    dve.wait_ge(a.proj_done, t + 1)
                    nc.vector.scalar_tensor_tensor(x[:, t, :], bank[7][:, 256:512], tg[:, 1:2], xb[:],
                                                   ALU.mult, ALU.add).then_inc(a.x_done, 1)

                def next_wait(t):
                    dve.wait_ge(a.x_done, t + 1)
                    after(dve, m.xn_ready, t)

                def next_stats(t):
                    chain.mark(nc.vector.bn_stats(stats2[:], x[:, t, :]))

                def next_mean(t):
                    chain.link(nc.vector.bn_aggr(mv2[:], stats2[:]))
                    nc.vector.tensor_scalar(ve2[:], mv2[:, 1:2], EPS, None, ALU.add).then_inc(m.var_ready, 1)

                def next_apply(t):
                    dve.wait_ge(m.rstd_ready, t + 1)
                    after(dve, m.xt_done, t)
                    nc.vector.tensor_scalar(xm[:], x[:, t, :], mv2[:, 0:1], rstd2[:], ALU.subtract, ALU.mult
                                            ).then_inc(m.xn_ready, 1)

                def nothing():
                    pass

                def body0(t):
                    n = a.units * t
                    stats_of = t - 2 if live(t - 2) else None

                    def sequence_before(b2, stats_of=None):
                        if live(t - 1):
                            normalise(t - 1, b2, stats_of)
                        elif stats_of is not None:
                            next_wait(stats_of)
                            next_stats(stats_of)
                            chain.wait()

                    between = [nothing, lambda: sequence_before(0, stats_of),
                               (lambda: layer_norm(a, t + 2)) if live(t + 2) else nothing, lambda: sequence_before(1)]
                    for u in range(4):
                        if live(t):
                            shift(n + u, u % 2, between[u])
                        else:
                            between[u]()
                        if u == 1 and stats_of is not None:
                            next_mean(stats_of)
                        if u == 2 and stats_of is not None:
                            next_apply(stats_of)

                def body1(t):
                    n = a.units * t
                    late = isinstance(t, int) and t == 0
                    if live(t):
                        shift(n, 0, (lambda: layer_norm(a, t + 2)) if live(t + 2) and not late else nothing)
                    if late:
                        layer_norm(a, t + 2)
                    if live(t - 3):
                        next_apply(t - 3)
                    if live(t - 1):
                        normalise(t - 1, 0)
                    if live(t):
                        shift(n + 1, 1, nothing)
                    if live(t - 2):
                        residual(t - 2)
                    stats_of = t - 2 if live(t - 2) else None
                    if live(t - 1):
                        normalise(t - 1, 1, stats_of)
                    elif stats_of is not None:
                        next_wait(stats_of)
                        next_stats(stats_of)
                        chain.wait()
                    if stats_of is not None:
                        next_mean(stats_of)

                body = body0 if a.layer == 0 else body1

                for part, (t0, t1) in enumerate(((0, AHEAD), (AHEAD, TT))):
                    if before is None:
                        dve.wait_ge(x_loaded[part], 16)
                    if before is None or part == 1:
                        ln_stats(a, before, t0, t1)
                    if part == 0:
                        if before is None:
                            dve.wait_ge(a.rstd_ready, 1)
                            layer_norm(a, 0)
                            dve.wait_ge(v_zeroed, 2)
                            value_ones(dve, nc.vector, a)
                            dve.wait_ge(k_loaded, 48)
                            for r, ready in enumerate((kh_ready, kl_ready)):
                                dve.wait_ge(ready, 1)
                                keys(nc.vector, a, 0, r, k0_ready)
                            layer_norm(a, 1)
                        else:
                            layer_norm(a, 1)
                for t in range(a.lag):
                    body(t)
                at0 = chain.n
                links = a.units + 4
                with dve.Fori(a.lag, TT - AHEAD) as t:
                    chain.at(at0 + (t - a.lag) * links)
                    body(t)
                    assert chain.n == links
                chain.at(at0 + (TT - AHEAD - a.lag) * links)
                for t in range(TT - AHEAD, TT + a.lag):
                    body(t)

            def feed_forward(m, before):
                chain = Chain(dve, R.chain)

                def multiply(n, k):
                    dve.wait_ge(m.s_ready, n + 1)
                    dve.wait_ge(m.u_done, n + 1)
                    nc.vector.tensor_tensor(t_t[:], bank[2 + k][:], s_t[:, k, :], ALU.mult).then_inc(m.t_done, 1)

                def weigh(n, q, k):
                    dve.wait_ge(m.t_done, n + 1)
                    nc.vector.tensor_tensor(h_t[:, k, :], t_t[:], mbc[:, q, k * BLK:(k + 1) * BLK], ALU.mult
                                            ).then_inc(m.h_full, 1)

                def split_h(n, k):
                    dve.wait_ge(m.hh_ready, n + 1)
                    nc.vector.tensor_tensor(hl[:, k, :], h_t[:, k, :], hh[:, k, :].bitcast(F32), ALU.subtract
                                            ).then_inc(m.h_split, 1)

                if m.layer == 0:
                    dve.wait_ge(w_const, 16 * 7)
                    nc.vector.tensor_scalar(sdt[:], sd[:], tg[:, 2:3], None, ALU.mult).then_inc(sdt_ready, 1)
                    nc.vector.tensor_scalar(bcb[:], bcb[:], tg[:, 1:2], None, ALU.mult).then_inc(bcb_ready, 1)
                    nc.vector.tensor_copy(gwh[:], gw[:]).then_inc(R.gw_split, 1)
                    dve.wait_ge(R.gw_split, 1)
                    nc.vector.tensor_tensor(gwl[:], gw[:], gwh[:].bitcast(F32), ALU.subtract).then_inc(R.gw_split, 1)
                else:
                    dve.wait_ge(R.sel_loaded, 16)
                    nc.vector.tensor_copy(sel, sel_raw).then_inc(R.sel_ready, 1)
                    dve.wait_ge(R.logits_done, 1)
                    chain.link(nc.vector.tensor_copy(lg, bank[4][:, 2 * P:4 * P].rearrange(
                        "p (t e) -> p t e", e=EXPERTS)))
                    for t in range(TT):
                        last = nc.vector.max(top[:, t, :], lg[:, t, :])
                    chain.link(last)
                    nc.vector.tensor_tensor(ew, lg, top[:, :, 0:1].to_broadcast([P, TT, EXPERTS]),
                                            ALU.subtract).then_inc(R.d_ready, 1)
                    for t in range(TT):
                        last = nc.vector.match_replace(rep[:, t, :], top[:, t, :], lg[:, t, :], NEG)
                    chain.link(last)
                    chain.link(nc.vector.tensor_tensor(rep, rep, lg, ALU.not_equal))
                    dve.wait_ge(R.e_ready, 1)
                    chain.link(nc.vector.tensor_tensor(ew, ew, rep, ALU.mult))
                    chain.link(nc.vector.reduce_sum(esum[:], ew, AX.X))
                    chain.link(nc.vector.reciprocal(esum[:], esum[:]))
                    nc.vector.tensor_tensor(ew, ew, esum[:].unsqueeze(2).to_broadcast([P, TT, EXPERTS]),
                                            ALU.mult).then_inc(R.w_ready, 1)
                    multiply(0, 0)
                    for k in range(NBLK):
                        dve.wait_ge(R.wt_hi, k + 1)
                        cols = slice(k * BLK, (k + 1) * BLK)
                        nc.vector.tensor_tensor(wts[EXPERTS:2 * EXPERTS, cols], bank[5 + k][0:EXPERTS, :],
                                                wts[0:EXPERTS, cols].bitcast(F32), ALU.subtract
                                                ).then_inc(R.wt_lo, 1)

                    def mask_out(j):
                        dve.wait_ge(R.spread_done, j + 1)
                        nc.vector.tensor_copy(mask(j), bank[MASK_BANKS[j % 4]][:]).then_inc(R.mask_ready[1], 1)

                    mask_out(1)
                    dve.wait_ge(R.mask_ready[0], 1)
                    weigh(0, 0, 0)
                    dve.wait_ge(m.h_full, 1)
                    multiply(1, 1)
                    dve.wait_ge(R.mask_ready[1], 1)
                    weigh(1, 0, 1)
                    mask_out(5)
                    split_h(0, 0)
                    split_h(1, 1)
                    mask_out(9)
                    mask_out(13)

                def body(i, first):
                    for cc in range(m.per_body):
                        c = i * m.per_body + cc
                        for k in range(NBLK):
                            n = NBLK * c + k
                            if m.layer == 0:
                                dve.wait_ge(m.s_ready, n + 1)
                                dve.wait_ge(m.u_done, n + 1)
                                nc.vector.scalar_tensor_tensor(h_t[:, k, :], bank[2 + k][:], su[:, c:c + 1],
                                                               s_t[:, k, :], ALU.mult, ALU.mult
                                                               ).then_inc(m.t_done, 1)
                                dve.wait_ge(m.t_done, n + 1)
                            elif not (first and cc == 0):
                                multiply(n, k)
                                weigh(n, i * (m.per_body // CPQ) + cc // CPQ, k)
                            if not (m.layer == 1 and first and cc == 0):
                                split_h(n, k)

                body(0, True)
                if m.chunks > m.per_body:
                    with dve.Fori(1, m.chunks // m.per_body) as i:
                        body(i, False)
                def add_back(t0, t1):
                    for t in range(t0, t1):
                        dve.wait_ge(m.back_done, t + 1)
                        nc.vector.tensor_tensor(x[:, t, :], bank[t % 4][:, 0:DM], x[:, t, :], ALU.add
                                                ).then_inc(m.x_done, 1)

                ahead = AHEAD if m.layer == 0 else 0
                add_back(0, ahead)
                if m.layer == 0:
                    ln_stats(A[1], m, 0, ahead)
                dve.wait_ge(m.dn_done, NBLK * m.chunks)
                scale = sdt[:, 1:2] if m.layer == 0 else tg[:, 3:4]
                nc.vector.tensor_scalar(ot[:, 1, BLK:2 * BLK], bank[7][:], scale, None, ALU.mult
                                        ).then_inc(m.ot_ready[1], 1)
                if m.layer == 0:
                    dve.wait_ge(A[1].rstd_ready, 1)
                    layer_norm(A[1], 0)
                add_back(ahead, TT)

            attention(A[0], M[0], None)
            feed_forward(M[0], A[0])
            attention(A[1], M[1], M[0])
            feed_forward(M[1], A[1])

        @block.tensor
        def _(pe):
            def product(o, w_sl, s, rh, rl, first, last, reopened=False):
                nc.tensor.matmul(o, wh[:, s, w_sl], rh, start=first, stop=False, skip_group_check=reopened)
                nc.tensor.matmul(o, wh[:, s, w_sl], rl, start=False, stop=False, skip_group_check=reopened)
                return nc.tensor.matmul(o, wl[:, s, w_sl], rh, start=False, stop=last, skip_group_check=reopened)

            def gate_up(m, n, c, s, k, fresh, which=None):
                if k == 0:
                    pe.wait_ge(m.w_split, c + 1)
                tok = slice(k * BLK, (k + 1) * BLK)
                both = ((0, k, m.s_ready, m.g_done), (DM, 2 + k, m.t_done, m.u_done))
                for col, bk, free, done in both if which is None else both[which:which + 1]:
                    if not fresh:
                        pe.wait_ge(free, n - 1)
                    for h in range(KC):
                        last = product(bank[bk][:], slice(col + h * P, col + (h + 1) * P), s, xh[:, h, tok],
                                       xl[:, h, tok], h == 0, h == KC - 1)
                    last.then_inc(done, 1)

            def route_logits(m, t0, t1):
                for t in range(t0, t1):
                    pe.wait_ge(m.xt_split, t + 1)
                    tok = slice(t * P, (t + 1) * P)
                    for k in range(KC):
                        for i, (xs, ws) in enumerate(((xh, gwh), (xh, gwl), (xl, gwh))):
                            last = nc.tensor.matmul(bank[4][:, 2 * P + t * EXPERTS:2 * P + (t + 1) * EXPERTS], xs[:, k, tok],
                                                    ws[:, k, :], start=(k == 0 and i == 0),
                                                    stop=(k == KC - 1 and i == 2))
                if t1 == TT:
                    last.then_inc(R.logits_done, 1)

            def attention(a, m):
                def q_transposes(t):
                    pe.wait_ge(a.q_split, t + 1)
                    after(pe, a.q_ready, t)
                    if a.layer == 1:
                        after(pe, m.xtf_ready, t - 4)
                    for g in range(G):
                        last = nc.tensor.transpose(bank[6][:, g * P:(g + 1) * P],
                                                   qs[:, g, :, :].rearrange("p r d -> p (r d)").bitcast(F32), ident[:])
                    last.then_inc(a.q_transposed, 1)

                def scores(n, t, u):
                    if u == 0:
                        if a.layer == 0:
                            after(pe, a.k_ready, 2 * t)
                        else:
                            pe.wait_ge(a.k_ready, 2 * (t + 1))
                        pe.wait_ge(a.q_ready, t + 1)
                    after(pe, a.sub_done, n - 1)
                    b2, gps = a.unit(u)
                    for i, gp in enumerate(gps):
                        for r in range(2):
                            last = nc.tensor.matmul(bank[u % 2][:, i * a.ns:(i + 1) * a.ns],
                                                    qt[:, b2, 2 * gp:2 * gp + 2, :].rearrange("p g s -> p (g s)"),
                                                    a.kbd[:, r, 2 * t + b2, :], start=(r == 0), stop=(r == 1))
                    last.then_inc(a.scored, 1)

                def p_transposes(n, k):
                    pe.wait_ge(a.p_ready, n + 1)
                    after(pe, a.pts_ready, 2 * (n - 1))
                    for j in range(4):
                        last = nc.tensor.transpose(bank[2 + k][:, j * P:(j + 1) * P], pt[:, k, j * P:(j + 1) * P],
                                                   ident[:])
                    last.then_inc(a.pt_done, 1)

                def values(n, t, u):
                    k = u % 2
                    b2, gps = a.unit(u)
                    pe.wait_ge(a.pts_ready, 2 * n + 1)
                    after(pe, a.y_done, 2 * t + b2 - 1)
                    if a.layer == 1 and b2 == 0 and isinstance(t, int) and t >= TT - 2:
                        route_logits(m, 0 if t == TT - 2 else t - 4, t - 3)
                    for j in range(4):
                        gp, pair = gps[j // a.npair], j % a.npair
                        if j == 2:
                            pe.wait_ge(a.pts_ready, 2 * (n + 1))
                        last = nc.tensor.matmul(bank[4 + b2][:, gp * P:(gp + 1) * P], pts[:, k, j, :],
                                                a.vbd[:, 2 * t + b2, pair, :], start=(pair == 0),
                                                stop=(pair == a.npair - 1))
                    last.then_inc(a.av_done, 1)

                def y_transposes(t):
                    pe.wait_ge(a.y_done, 2 * (t + 1))
                    after(pe, a.x_done, t)
                    for k in range(KC):
                        last = nc.tensor.transpose(bank[7][:, k * P:(k + 1) * P], yt[:, k * P:(k + 1) * P], ident[:])
                    last.then_inc(a.yt_done, 1)

                def project(t):
                    pe.wait_ge(a.yts_ready, t + 1)
                    o = bank[7][:, 256:512]
                    for k in range(KC):
                        last = nc.tensor.matmul(o, yts[:, k, :], wc[:, k, :], start=(k == 0), stop=(k == KC - 1))
                    last.then_inc(a.proj_done, 1)

                def x_transposes(t):
                    pe.wait_ge(m.xn_ready, t + 1)
                    if a.layer == 1:
                        pe.wait_ge(a.q_ready, up_to(t + 5, TT))
                    after(pe, m.xtf_ready, t)
                    for k in range(KC):
                        last = nc.tensor.transpose(bank[a.x_bank][:, k * P:(k + 1) * P], xm[:, k * P:(k + 1) * P],
                                                   ident[:])
                    last.then_inc(m.xt_done, 1)

                def first_product(t):
                    if isinstance(t, int) and t > TT and t < TT + 3:
                        pe.wait_ge(m.xt_split, TT // 2)
                        gate_up(m, 0, 0, 0, 0, True, t - TT - 1)

                def body(t):
                    if a.layer == 0:
                        first_product(t)
                    for u in range(a.units):
                        n = a.units * t + u
                        ahead = t if u + 2 < a.units else t + 1
                        if live(ahead) and live(t):
                            scores(n + 2, ahead, (u + 2) % a.units)
                        if a.layer == 1 and u == 0 and live(t - 2):
                            project(t - 2)
                        if a.layer == 0 and u == 1 and live(t + 1):
                            q_transposes(t + 1)
                        if a.layer == 0 and u == 3 and live(t - 2):
                            x_transposes(t - 2)
                        if a.layer == 1 and u == 0 and live(t - 3):
                            x_transposes(t - 3)
                        if a.layer == 1 and u == 1 and live(t + 2):
                            q_transposes(t + 2)
                        past = 2 if a.layer == 0 else 1
                        tile = t if u >= past else t - 1
                        if live(tile):
                            values(n - past, tile, (u - past) % a.units)
                        if live(t):
                            p_transposes(n, u % 2)
                        if a.layer == 1 and u == 1 and live(t - 1):
                            y_transposes(t - 1)
                    if a.layer == 1 and isinstance(t, int) and t >= TT:
                        pe.wait_ge(a.y_done, 2 * TT)
                        route_logits(m, t - 4, t - 3)
                    if a.layer == 1:
                        first_product(t)

                q_transposes(0)
                if a.layer == 0:
                    pe.wait_ge(k0_ready, 2)
                if a.layer == 1:
                    pe.wait_ge(M[0].x_done, TT)
                scores(0, 0, 0)
                scores(1, 0, 1)
                if a.layer == 1:
                    q_transposes(1)
                pe.wait_ge(a.v_ready, 2 * a.hk)
                over_tiles(pe, a.lag, body)

            def feed_forward(m):
                def route_weights():
                    pe.wait_ge(R.w_ready, 1)
                    for t in range(TT):
                        last = nc.tensor.transpose(bank[5 + t // 4][0:EXPERTS, (t % 4) * P:(t % 4 + 1) * P],
                                                   ew[:, t, :], ident[:])
                    last.then_inc(R.wt_done, 1)

                def spread_weights():
                    pe.wait_ge(R.sel_ready, 1)
                    pe.wait_ge(R.wt_lo, NBLK)
                    for j in range(MASKS):
                        if j >= 4:
                            pe.wait_ge(R.mask_ready[on_vector(j - 4)], masks_out(j - 4))
                        q, k = j // NBLK, j % NBLK
                        nc.tensor.matmul(bank[MASK_BANKS[j % 4]][:], sel[:, q * P:(q + 1) * P],
                                         wts[:, k * BLK:(k + 1) * BLK], start=True, stop=True
                                         ).then_inc(R.spread_done, 1)
                    for j in range(MASKS - 4, MASKS):
                        pe.wait_ge(R.mask_ready[on_vector(j)], masks_out(j))

                def down(n, s, k, first):
                    pe.wait_ge(m.h_split, n + 1)
                    for h in range(KC):
                        ins = product(bank[4 + 2 * h + k][:], slice(2 * DM + h * P, 2 * DM + (h + 1) * P), s,
                                      hh[:, k, :], hl[:, k, :], first, True, reopened=True)
                    ins.then_inc(m.dn_done, 1)

                def body(i, first):
                    for cc in range(m.per_body):
                        c = i * m.per_body + cc
                        for k in range(NBLK):
                            n = NBLK * c + k
                            if first and n == 0:
                                continue
                            if first and n == 1:
                                pe.wait_ge(m.xt_split, TT)
                            if not (m.layer == 1 and first and n == 2):
                                gate_up(m, n, c, cc % WRING, k, first and cc == 0)
                            if m.layer == 1 and first and n == 1:
                                route_weights()
                                gate_up(m, 2, 1, 1, 0, False)
                                spread_weights()
                            if first and n == 1:
                                down(0, 0, 0, True)
                                continue
                            if not (first and n == 0):
                                down(n - 1, (cc if k else cc - 1) % WRING, 1 - k, first and n <= 2)
                body(0, True)
                if m.chunks > m.per_body:
                    with pe.Fori(1, m.chunks // m.per_body) as i:
                        body(i, False)
                def back(t0, t1):
                    for t in range(t0, t1):
                        pe.wait_ge(m.ot_ready[t // 4], KC)
                        if t >= 4:
                            pe.wait_ge(m.x_done, t - 3)
                        for h in range(KC):
                            last = nc.tensor.transpose(bank[t % 4][:, h * P:(h + 1) * P],
                                                       ot[:, h, t * P:(t + 1) * P], ident[:])
                        last.then_inc(m.back_done, 1)

                ahead = AHEAD if m.layer == 0 else 0
                back(0, ahead)
                down(NBLK * m.chunks - 1, (m.chunks - 1) % WRING, 1, False)
                back(ahead, TT)

            pe.wait_ge(c_loaded, 16 * 3)
            attention(A[0], M[0])
            pe.wait_ge(w_const, 16 * 7)
            feed_forward(M[0])
            attention(A[1], M[1])
            feed_forward(M[1])



def kernel(x, ctx_512, g_xattn, g_ffn, L0_ffn_wq_gate, L0_ffn_s_gate, L0_ffn_wq_up, L0_ffn_s_up, L0_ffn_wq_down,
           L0_ffn_s_down, L1_xattn_Wc, L1_xattn_bc, L1_ffn_gate_w, L1_ffn_w_gate_proj, L1_ffn_w_up_proj,
           L1_ffn_w_down_proj):
    import numpy as np
    import concourse.bacc as bacc
    from concourse import mybir as mb
    from concourse.bass_utils import run_bass_kernel_spmd as run

    A = np.asarray

    def halves(rows, n):
        return rows.reshape(n, P, KC, P).transpose(0, 3, 2, 1).reshape(n, P, DM)

    def own_rows(heads):
        return np.tile(np.repeat(np.eye(heads, dtype=np.float32), 64 // heads, axis=0), (2, 1))

    pad = FFN_CHUNKS * P - HIDDEN
    gate0 = np.pad(A(L0_ffn_wq_gate), ((0, pad), (0, 0)))
    up0 = np.pad(A(L0_ffn_wq_up), ((0, pad), (0, 0)))
    down0 = np.pad(A(L0_ffn_wq_down).T, ((0, pad), (0, 0)))
    w0 = np.concatenate([halves(gate0, FFN_CHUNKS), halves(up0, FFN_CHUNKS), down0.reshape(FFN_CHUNKS, P, DM)], 2)
    s_gate = np.pad(A(L0_ffn_s_gate), (0, pad)).reshape(FFN_CHUNKS, P).T
    s_up = np.pad(A(L0_ffn_s_up), (0, pad)).reshape(FFN_CHUNKS, P).T

    def rows(w):
        return w.reshape(EXPERTS // EPQ, EPQ, CPQ, 32, DM).transpose(0, 2, 1, 3, 4).reshape(MOE_CHUNKS * P, DM)
    w1 = np.concatenate([halves(rows(A(L1_ffn_w_gate_proj)), MOE_CHUNKS), halves(rows(A(L1_ffn_w_up_proj)), MOE_CHUNKS),
                         rows(A(L1_ffn_w_down_proj).transpose(0, 2, 1)).reshape(MOE_CHUNKS, P, DM)], 2)
    ctx = A(ctx_512)
    ins = {
        "x_in": A(x).reshape(TOK, DM),
        "ctx_t": ctx.transpose(2, 0, 1).reshape(64, BATCH * KEYS),
        "ctx_in": ctx,
        "g_xattn": A(g_xattn),
        "g_ffn": A(g_ffn),
        "w0": w0,
        "s_gate": s_gate,
        "s_up": s_up,
        "s_down": A(L0_ffn_s_down).reshape(KC, P).T,
        "wc_t": A(L1_xattn_Wc).T,
        "bc": A(L1_xattn_bc),
        "gate_t": A(L1_ffn_gate_w).T,
        "w1": w1,
        "ident_in": np.eye(P, dtype=np.float32),
        "kmask0": own_rows(8),
        "kmask1": own_rows(4),
        "sel_in": np.tile(np.repeat(np.eye(EXPERTS, dtype=np.float32), 32, axis=1), (2, 1)),
    }
    nc = bacc.Bacc("TRN2", target_bir_lowering=False, num_devices=1)
    arrays, args = {}, []
    for name, a in ins.items():
        a = np.ascontiguousarray(a)
        arrays[name] = a
        args.append(nc.dram_tensor(name, a.shape, mb.dt.from_np(a.dtype), kind="ExternalInput").ap())
    args.append(nc.dram_tensor("out", (TOK, DM), F32, kind="ExternalOutput").ap())
    build(nc, *args)
    r = run(nc, [arrays], core_ids=[0])
    return r.results[0]["out"].reshape(BATCH, SEQ, DM)
```
